# Optimizing a Trainium2 kernel written in Bass

```python
import numpy as np
import jax
import jax.numpy as jnp

def _softmax(x, axis=-1):
    return jax.nn.softmax(x, axis=axis)

def _gelu(x):
    return jax.nn.gelu(x, approximate=True)

def _silu(x):
    return jax.nn.silu(x)

def _sigmoid(x):
    return jax.nn.sigmoid(x)

def _layernorm(x, axis=-1, eps=1e-05):
    m = jnp.mean(x, axis=axis, keepdims=True)
    v = jnp.var(x, axis=axis, keepdims=True)
    return (x - m) / jnp.sqrt(v + eps)

def _scatter_add(tgt, idx, src, axis=0):
    return tgt.at[idx].add(src)

def _segment_sum(src, seg, n):
    return jax.ops.segment_sum(src, seg, n)
kernel_name = 'mk_lm_tower_d1_tok_ids1024_r4_f59bf0'

def setup_inputs(seed: int=0):
    np.random.seed(seed)
    _w = jnp.asarray

    def _rec_inputs():
        import jax
        import jax.numpy as jnp
        _rk = jax.random.key(seed)
        x = jax.random.randint(jax.random.fold_in(_rk, 1), (16, 128), 0, 31999, jnp.int32)
        return x
    x = _rec_inputs()

    def _L0_tok_setup():
        import jax, jax.numpy as jnp
        import numpy as np
        VOCAB = 8000
        EMBED = 256
        RANK = 16
        ALPHA = 16
        SCALING = ALPHA / RANK
        key = jax.random.key(seed)
        k_x, k_w, k_a = jax.random.split(key, 3)
        x = jax.random.randint(k_x, (4, 1024), 0, VOCAB, dtype=jnp.int32)
        base_weight = jax.random.normal(k_w, (EMBED, VOCAB), dtype=jnp.float32) * 0.02
        lora_A = jax.random.normal(k_a, (VOCAB, RANK), dtype=jnp.float32) * 0.02
        lora_B = jnp.zeros((RANK, EMBED), dtype=jnp.float32)
        return {'x': x, 'base_weight': base_weight, 'lora_A': lora_A, 'lora_B': lora_B}
    _L0_tok_all = _L0_tok_setup()
    _L0_tok_in = {k: v for k, v in _L0_tok_all.items() if k in ('base_weight', 'lora_A', 'lora_B')}
    del _L0_tok_all

    def _L0_attn_setup():
        import jax, jax.numpy as jnp
        import numpy as np
        NUM_HEADS = 4
        CHUNK = 64
        GATE_NORM = 16.0
        EPS = 1e-05

        def _xavier(key, fan_in, fan_out):
            gain = 2.0 ** (-2.5)
            limit = gain * np.sqrt(6.0 / (fan_in + fan_out))
            return jax.random.uniform(key, (fan_in, fan_out), jnp.float32, -limit, limit)

        def _to_chunks(t, B, H, NC, C):
            d = t.shape[-1]
            return t.reshape(B, H, NC, C, d).transpose(2, 0, 1, 3, 4)

        def _gla_forward(x, Wq, Wk, Wv, Wg, gk_w1, gk_w2, gk_b2, g_norm_w, Wo):
            B, L, D = x.shape
            H = NUM_HEADS
            C = CHUNK
            NC = L // C
            q = x @ Wq
            k = x @ Wk
            v = x @ Wv
            gk = jax.nn.log_sigmoid(x @ gk_w1 @ gk_w2 + gk_b2) / GATE_NORM

            def split_heads(t):
                return t.reshape(B, L, H, -1).transpose(0, 2, 1, 3)
            q, k, v, gk = map(split_heads, (q, k, v, gk))
            dk = q.shape[-1]
            scale = dk ** (-0.5)
            qc = _to_chunks(q, B, H, NC, C)
            kc = _to_chunks(k, B, H, NC, C)
            vc = _to_chunks(v, B, H, NC, C)
            gc = _to_chunks(gk, B, H, NC, C)
            Bcum = jnp.cumsum(gc, axis=3)
            causal = jnp.tril(jnp.ones((C, C), jnp.float32))

            def step(Hst, inp):
                qi, ki, vi, bi = inp
                qg = qi * jnp.exp(bi) * scale
                kg = ki * jnp.exp(-bi)
                o_inter = jnp.einsum('bhcd,bhde->bhce', qg, Hst)
                A = jnp.einsum('bhtd,bhsd->bhts', qg, kg) * causal
                o_intra = jnp.einsum('bhts,bhse->bhte', A, vi)
                b_last = bi[:, :, -1:, :]
                kH = ki * jnp.exp(b_last - bi)
                H_new = jnp.exp(b_last).transpose(0, 1, 3, 2) * Hst + jnp.einsum('bhcd,bhce->bhde', kH, vi)
                return (H_new, o_inter + o_intra)
            dv = v.shape[-1]
            H0 = jnp.zeros((B, H, dk, dv), jnp.float32)
            _, oc = jax.lax.scan(step, H0, (qc, kc, vc, Bcum))
            o = oc.transpose(1, 2, 0, 3, 4).reshape(B, H, L, dv)
            o = o.transpose(0, 2, 1, 3)
            rms = jnp.sqrt(jnp.mean(o * o, axis=-1, keepdims=True) + EPS)
            o_n = o / rms * g_norm_w
            g = (x @ Wg).reshape(B, L, H, dv)
            o = o_n * g * jax.nn.sigmoid(g)
            return o.reshape(B, L, H * dv) @ Wo
        key = jax.random.key(seed)
        ks = jax.random.split(key, 8)
        B, L, D = (4, 512, 256)
        Dk, Dv, R = (256, 512, 16)
        x = jax.random.normal(ks[0], (B, L, D), jnp.float32)
        return {'x': x, 'Wq': _xavier(ks[1], D, Dk), 'Wk': _xavier(ks[2], D, Dk), 'Wv': _xavier(ks[3], D, Dv), 'Wg': _xavier(ks[4], D, Dv), 'gk_w1': _xavier(ks[5], D, R), 'gk_w2': _xavier(ks[6], R, Dk), 'gk_b2': jnp.zeros((Dk,), jnp.float32), 'g_norm_w': jnp.ones((Dv // NUM_HEADS,), jnp.float32), 'Wo': _xavier(ks[7], Dv, D)}
    _L0_attn_all = _L0_attn_setup()
    _L0_attn_in = {k: v for k, v in _L0_attn_all.items() if k in ('Wq', 'Wk', 'Wv', 'Wg', 'gk_w1', 'gk_w2', 'gk_b2', 'g_norm_w', 'Wo')}
    del _L0_attn_all

    def _L0_ffn_setup():
        import jax, jax.numpy as jnp
        import numpy as np
        D_MODEL = 256
        D_FF = 704
        N_EXPERTS = 8
        key = jax.random.key(seed)
        k_in, k1, k2, k3 = jax.random.split(key, 4)
        scale = 0.02
        inputs = jax.random.normal(k_in, (4, N_EXPERTS * 512, D_MODEL), dtype=jnp.float32)
        w1 = jax.random.normal(k1, (N_EXPERTS, D_MODEL, D_FF), dtype=jnp.float32) * scale
        w3 = jax.random.normal(k3, (N_EXPERTS, D_MODEL, D_FF), dtype=jnp.float32) * scale
        w2 = jax.random.normal(k2, (N_EXPERTS, D_FF, D_MODEL), dtype=jnp.float32) * scale
        return {'inputs': inputs, 'w1': w1, 'w3': w3, 'w2': w2}
    _L0_ffn_all = _L0_ffn_setup()
    _L0_ffn_in = {k: v for k, v in _L0_ffn_all.items() if k in ('w1', 'w3', 'w2')}
    del _L0_ffn_all
    return {'x': x, 'L0_tok_base_weight': _L0_tok_in['base_weight'], 'L0_tok_lora_A': _L0_tok_in['lora_A'], 'L0_tok_lora_B': _L0_tok_in['lora_B'], 'L0_attn_Wq': _L0_attn_in['Wq'], 'L0_attn_Wk': _L0_attn_in['Wk'], 'L0_attn_Wv': _L0_attn_in['Wv'], 'L0_attn_Wg': _L0_attn_in['Wg'], 'L0_attn_gk_w1': _L0_attn_in['gk_w1'], 'L0_attn_gk_w2': _L0_attn_in['gk_w2'], 'L0_attn_gk_b2': _L0_attn_in['gk_b2'], 'L0_attn_g_norm_w': _L0_attn_in['g_norm_w'], 'L0_attn_Wo': _L0_attn_in['Wo'], 'L0_ffn_w1': _L0_ffn_in['w1'], 'L0_ffn_w3': _L0_ffn_in['w3'], 'L0_ffn_w2': _L0_ffn_in['w2']}

def reference(x, L0_tok_base_weight, L0_tok_lora_A, L0_tok_lora_B, L0_attn_Wq, L0_attn_Wk, L0_attn_Wv, L0_attn_Wg, L0_attn_gk_w1, L0_attn_gk_w2, L0_attn_gk_b2, L0_attn_g_norm_w, L0_attn_Wo, L0_ffn_w1, L0_ffn_w3, L0_ffn_w2):
    import jax
    import jax.numpy as jnp

    def _L0_tok_ref(x, base_weight, lora_A, lora_B):
        import jax, jax.numpy as jnp
        import numpy as np
        VOCAB = 8000
        EMBED = 256
        RANK = 16
        ALPHA = 16
        SCALING = ALPHA / RANK
        x_emb = base_weight.T[x]
        lora = jnp.einsum('bsr,re->bse', lora_A[x], lora_B)
        return x_emb + lora * SCALING

    def _L0_attn_ref(x, Wq, Wk, Wv, Wg, gk_w1, gk_w2, gk_b2, g_norm_w, Wo):
        import jax, jax.numpy as jnp
        import numpy as np
        NUM_HEADS = 4
        CHUNK = 64
        GATE_NORM = 16.0
        EPS = 1e-05

        def _xavier(key, fan_in, fan_out):
            gain = 2.0 ** (-2.5)
            limit = gain * np.sqrt(6.0 / (fan_in + fan_out))
            return jax.random.uniform(key, (fan_in, fan_out), jnp.float32, -limit, limit)

        def _to_chunks(t, B, H, NC, C):
            d = t.shape[-1]
            return t.reshape(B, H, NC, C, d).transpose(2, 0, 1, 3, 4)

        def _gla_forward(x, Wq, Wk, Wv, Wg, gk_w1, gk_w2, gk_b2, g_norm_w, Wo):
            B, L, D = x.shape
            H = NUM_HEADS
            C = CHUNK
            NC = L // C
            q = x @ Wq
            k = x @ Wk
            v = x @ Wv
            gk = jax.nn.log_sigmoid(x @ gk_w1 @ gk_w2 + gk_b2) / GATE_NORM

            def split_heads(t):
                return t.reshape(B, L, H, -1).transpose(0, 2, 1, 3)
            q, k, v, gk = map(split_heads, (q, k, v, gk))
            dk = q.shape[-1]
            scale = dk ** (-0.5)
            qc = _to_chunks(q, B, H, NC, C)
            kc = _to_chunks(k, B, H, NC, C)
            vc = _to_chunks(v, B, H, NC, C)
            gc = _to_chunks(gk, B, H, NC, C)
            Bcum = jnp.cumsum(gc, axis=3)
            causal = jnp.tril(jnp.ones((C, C), jnp.float32))

            def step(Hst, inp):
                qi, ki, vi, bi = inp
                qg = qi * jnp.exp(bi) * scale
                kg = ki * jnp.exp(-bi)
                o_inter = jnp.einsum('bhcd,bhde->bhce', qg, Hst)
                A = jnp.einsum('bhtd,bhsd->bhts', qg, kg) * causal
                o_intra = jnp.einsum('bhts,bhse->bhte', A, vi)
                b_last = bi[:, :, -1:, :]
                kH = ki * jnp.exp(b_last - bi)
                H_new = jnp.exp(b_last).transpose(0, 1, 3, 2) * Hst + jnp.einsum('bhcd,bhce->bhde', kH, vi)
                return (H_new, o_inter + o_intra)
            dv = v.shape[-1]
            H0 = jnp.zeros((B, H, dk, dv), jnp.float32)
            _, oc = jax.lax.scan(step, H0, (qc, kc, vc, Bcum))
            o = oc.transpose(1, 2, 0, 3, 4).reshape(B, H, L, dv)
            o = o.transpose(0, 2, 1, 3)
            rms = jnp.sqrt(jnp.mean(o * o, axis=-1, keepdims=True) + EPS)
            o_n = o / rms * g_norm_w
            g = (x @ Wg).reshape(B, L, H, dv)
            o = o_n * g * jax.nn.sigmoid(g)
            return o.reshape(B, L, H * dv) @ Wo
        return _gla_forward(x, Wq, Wk, Wv, Wg, gk_w1, gk_w2, gk_b2, g_norm_w, Wo)

    def _L0_ffn_ref(inputs, w1, w3, w2):
        import jax, jax.numpy as jnp
        import numpy as np
        D_MODEL = 256
        D_FF = 704
        N_EXPERTS = 8
        B, T, D = inputs.shape
        E = w1.shape[0]
        C = T // E
        x = inputs.reshape(B, E, C, D)
        gate = jnp.einsum('becd,edf->becf', x, w1)
        up = jnp.einsum('becd,edf->becf', x, w3)
        h = jax.nn.silu(gate) * up
        out = jnp.einsum('becf,efd->becd', h, w2)
        return out.reshape(B, T, D)
    h = _L0_tok_ref(x, L0_tok_base_weight, L0_tok_lora_A, L0_tok_lora_B)
    h = h + _L0_attn_ref(_layernorm(h, axis=-1), L0_attn_Wq, L0_attn_Wk, L0_attn_Wv, L0_attn_Wg, L0_attn_gk_w1, L0_attn_gk_w2, L0_attn_gk_b2, L0_attn_g_norm_w, L0_attn_Wo)
    h = h + _L0_ffn_ref(_layernorm(h, axis=-1), L0_ffn_w1, L0_ffn_w3, L0_ffn_w2)
    return h

_drawn_inputs = setup_inputs


def setup_inputs(seed=0):
    import zlib

    import numpy as np

    out = dict(_drawn_inputs(seed))
    spreads = {'L0_tok_lora_B': (0.0, 0.1), 'L0_attn_gk_b2': (0.0, 0.1), 'L0_attn_g_norm_w': (1.0, 0.2)}
    factors = {'L0_attn_gk_w1': 8.0, 'L0_attn_gk_w2': 4.924}
    for name, (base, spread) in spreads.items():
        noise = np.random.default_rng([zlib.crc32(name.encode()), seed]).standard_normal(out[name].shape)
        drawn = base * np.exp(spread * noise) if base else spread * noise
        out[name] = jnp.asarray(drawn.astype(out[name].dtype))
    for name, factor in factors.items():
        out[name] = (out[name] * factor).astype(out[name].dtype)
    return out
```

```python
import concourse.bass as bass
from concourse import mybir
from contextlib import ExitStack


B, S, D = 16, 128, 256
VOCAB, RANK = 8000, 16
H, DV, CHUNK = 4, 128, 64
DK = D // H
NV = H * DV
GATE_NORM, EPS = 16.0, 1e-5
E, F = 8, 704
P = 128
KT = D // P
TW = D + RANK
NP = B // 2
PT = 2 * S
FC = -(-F // P)
FT = F - (FC - 1) * P
POS = S // E
ET = B * POS
WCOLS = RANK + 2 * D + 2 * NV
WQK = RANK + 2 * D
C13 = KT * 2 * P
T13 = KT * 2 * FT
W13 = (FC - 1) * C13 + T13
HALF13 = FC // 2 * C13
RAW = W13 + FC * D
BLK = 32
LK = 2 * BLK + RANK + 1
TABLE_LN_EXP, TABLE_SILU = 6, 18


def need(eng, sem, count):
    if isinstance(count, int) and count <= 0:
        return
    eng.wait_ge(sem, count)


def wait_apart(eng, sem, count, passed):
    need(eng, sem, count)
    eng.sem_inc(passed, 1)


def least(count, top):
    return min(count, top) if isinstance(count, int) else count


def layer_kernel(nc, ids, table, w_attn, w_o, low_rank, g_norm, w13, w2_main, w2_tail,
                 scratch, out):
    f32, f32r, i32 = mybir.dt.float32, mybir.dt.float32r, mybir.dt.int32
    ALU, ACT, AX = mybir.AluOpType, mybir.ActivationFunctionType, mybir.AxisListType

    ctx = ExitStack()
    with ctx:
        def sb(name, shape, dt=f32):
            return ctx.enter_context(nc.sbuf_tensor(name, shape, dt))

        def sem(name):
            return ctx.enter_context(nc.semaphore(name))

        ident = sb("ident", [P, P])
        mask = sb("mask", [P, P])
        cum_w = sb("cum_w", [P, P])
        minus_half = sb("minus_half", [P, 8])
        lr_w = sb("lr_w", [3 * BLK, 2, D], f32r)
        gn_sb = sb("gn_sb", [P, 1])
        wa_hi = sb("wa_hi", [P, KT, WCOLS], f32r)
        wa_lo = sb("wa_lo", [P, KT, WCOLS], f32r)
        wo_hi = sb("wo_hi", [P, H, D], f32r)
        wo_lo = sb("wo_lo", [P, H, D], f32r)
        raw = [sb(f"raw{s}", [P, RAW]) for s in range(2)]
        e_hi = sb("e_hi", [P, RAW], f32r)
        e_lo = sb("e_lo", [P, RAW], f32r)
        ids_raw = sb("ids_raw", [P, B], i32)
        ids_f = sb("ids_f", [P, B])
        ids_ok = sb("ids_ok", [P, B], i32)
        ids_now = sb("ids_now", [P, 2], i32)
        G = sb("G", [P, 2, TW])
        Hres = sb("Hres", [P, B, D])
        stats = sb("stats", [P, 2, 6])
        mv = sb("mv", [P, 2, 2])
        veps = sb("veps", [P, 2])
        rstd = sb("rstd", [P, 2])
        stats2 = sb("stats2", [P, 2, 6])
        mv2 = sb("mv2", [P, 2, 2])
        veps2 = sb("veps2", [P, 2])
        rstd2 = sb("rstd2", [P, 2])
        xn = sb("xn", [P, 2, D])
        x_hi = sb("x_hi", [P, KT, PT], f32r)
        x_lo = sb("x_lo", [P, KT, PT], f32r)
        lr_x = sb("lr_x", [3 * BLK, 2, PT], f32r)
        v_sb = sb("v_sb", [P, 2, NV])
        sg = sb("sg", [P, 2, NV])
        lsig = sb("lsig", [P, 2 * D])
        gk = sb("gk", [P, 2, D])
        e_pos = sb("e_pos", [P, KT, PT])
        e_neg = sb("e_neg", [P, KT, PT])
        qg = sb("qg", [P, KT, PT])
        kg = sb("kg", [P, KT, PT])
        am = sb("am", [P, 2, 2, 2, P])
        sq = sb("sq", [P, NV])
        ss = sb("ss", [P, 2, H])
        ms = sb("ms", [P, 2, H])
        rr = sb("rr", [P, 2, H])
        og = sb("og", [P, 2, NV])
        o_hi = sb("o_hi", [P, 2, H, P], f32r)
        o_lo = sb("o_lo", [P, 2, H, P], f32r)
        xn2 = sb("xn2", [P, 2, D])
        x2_hi = sb("x2_hi", [P, E * KT * ET], f32r)
        x2_lo = sb("x2_lo", [P, E * KT * ET], f32r)

        s_act = am[:, :, :, :, :].rearrange("p a b c t -> p (a b c t)")
        h32 = og[:, :, :].rearrange("p a n -> p (a n)")
        h_hi = o_hi[:, :, :, :].rearrange("p a h t -> p (a h t)")
        h_lo = o_lo[:, :, :, :].rearrange("p a h t -> p (a h t)")
        lr_raw = sq[0:3 * BLK, :].rearrange("p (a n) -> p a n", a=2)
        y_out, h_res = v_sb, sg

        bank = [ctx.enter_context(nc.psum_tensor(f"bank{n}", [P, 512], f32)) for n in range(8)]
        q_ps, k_ps = bank[0], bank[1]
        xt_ps, xt2_ps = bank[3], bank[6]
        o_ps = [bank[3], bank[2]]
        a_ps = [bank[4], bank[5]]
        z_ps = cum_ps = bank[4]
        v_ps = bank[5]
        lr_ps = bank[6][0:RANK, :].rearrange("p (a n) -> p a n", a=2)
        lora_ps = wo_ps = bank[7]
        g_ps = [bank[7], bank[6]]
        gu_ps = [bank[0], bank[1], bank[2]]
        y_ps = [bank[3], bank[4]]

        ids_in, ids_done, consts, lr_in, wa_in, wa_rest_in, wo_in, gn_in = map(
            sem, ["ids_in", "ids_done", "consts", "lr_in", "wa_in", "wa_rest_in", "wo_in", "gn_in"])
        ids_sel = sem("ids_sel")
        gathered = [sem(f"gathered{t}") for t in range(2)]
        wa_hi_done, wa_lo_done, ones_done = sem("wa_hi_done"), sem("wa_lo_done"), sem("ones_done")
        lr_hi_done, lr_lo_done = sem("lr_hi_done"), sem("lr_lo_done")
        lrx_done, lrx_hi_done, lrx_dup_done, lrx_lo_done = (
            sem("lrx_done"), sem("lrx_hi_done"), sem("lrx_dup_done"), sem("lrx_lo_done"))
        lt_done, lora_done, h_done = sem("lt_done"), sem("lora_done"), sem("h_done")
        bn_done, mv_done, veps_done, rstd_done, xn_done = (
            sem("bn_done"), sem("mv_done"), sem("veps_done"), sem("rstd_done"), sem("xn_done"))
        xt_done, xhi_done, xlo_done = sem("xt_done"), sem("xhi_done"), sem("xlo_done")
        z_done = sem("z_done")
        abs_done, exp_done, ln_done, gk_done = sem("abs_done"), sem("exp_done"), sem("ln_done"), sem("gk_done")
        cum_done, epos_done, eneg_done = sem("cum_done"), sem("epos_done"), sem("eneg_done")
        q_done, k_done, qg_done, kg_done = sem("q_done"), sem("k_done"), sem("qg_done"), sem("kg_done")
        v_done, v_copied, g_done, silu_done = sem("v_done"), sem("v_copied"), sem("g_done"), sem("silu_done")
        a_done, am_done, pv_done = sem("a_done"), sem("am_done"), sem("pv_done")
        sq_done, ss_done, ms_done, rr_done = sem("sq_done"), sem("ss_done"), sem("ms_done"), sem("rr_done")
        og_done, ot_done, ohi_done, olo_done = sem("og_done"), sem("ot_done"), sem("ohi_done"), sem("olo_done")
        wo_done, h2_done, h2_stored = sem("wo_done"), sem("h2_done"), sem("h2_stored")
        bn2_done, mv2_done, veps2_done, rstd2_done, xn2_done = (
            sem("bn2_done"), sem("mv2_done"), sem("veps2_done"), sem("rstd2_done"), sem("xn2_done"))
        xt2_done, x2hi_done, x2lo_done = sem("xt2_done"), sem("x2hi_done"), sem("x2lo_done")
        raw13a_in, raw13b_in, raw2_in = (
            [sem(f"{part}_in{s}") for s in range(2)] for part in ("raw13a", "raw13b", "raw2"))
        w13_hi_done, w13_lo_done = sem("w13_hi_done"), sem("w13_lo_done")
        w2_hi_done, w2_lo_done = sem("w2_hi_done"), sem("w2_lo_done")
        up_done, act_done, mul_done, hhi_done, hlo_done, down_done = (
            sem("up_done"), sem("act_done"), sem("mul_done"), sem("hhi_done"), sem("hlo_done"), sem("down_done"))
        res_in = [sem(f"res_in{s}") for s in range(2)]
        y_done = sem("y_done")
        stored = [sem(f"stored{s}") for s in range(2)]

        dve_passed, pool_passed = sem("dve_passed"), sem("pool_passed")

        block = ctx.enter_context(nc.Block())

        def steps(eng, step):
            for i in (-1, 0, 1):
                step(i)
            with eng.Fori(2, NP - 1) as i:
                step(i)
            for i in (NP - 1, NP, NP + 1):
                step(i)

        def on(j):
            return not isinstance(j, int) or 0 <= j < NP

        def late(j):
            return isinstance(j, int) and j == NP - 1

        def gate_bank(j, t):
            return bank[t] if late(j) else g_ps[t]

        def rank_parts(i):
            parts = [p for p in range(2) if on(i + 1 - p)]
            return slice(parts[0], parts[-1] + 1) if parts else None

        def experts(eng, expert):
            expert(0, 0)
            expert(1, 1)
            with eng.Fori(1, E // 2) as pair:
                for s in range(2):
                    expert(pair * 2 + s, s)

        def chunk13(c):
            return (c * C13, C13 if c < FC - 1 else T13)

        def chunk2(c):
            return (W13 + c * D, D)

        def rows2(c):
            return P if c < FC - 1 else FT

        def first_chunk(i):
            return not isinstance(i, int) or 0 <= i - 2 < FC

        def first13(c):
            a, n = chunk13(c) if isinstance(c, int) else (c * C13, C13)
            return slice(a, a + n) if isinstance(c, int) else bass.ds(a, n)

        def first2(c):
            rows = slice(0, rows2(c) if isinstance(c, int) else P)
            return rows, slice(W13 + c * D, W13 + (c + 1) * D) if isinstance(c, int) else bass.ds(c * D + W13, D)

        def raw_count(e, s):
            return (e // 2 + 1) * 16 if isinstance(e, int) else (e - s) * 8 + 16

        def x2_view(x2, j):
            return x2[:, :].rearrange("p (e kt i j) -> p kt e i j", e=E, kt=2 * KT, i=POS)[:, :, :, :, bass.ds(j, 1)].rearrange(
                "p kt e i j -> p kt e (i j)")

        def xt2_src():
            return xt2_ps[:, :].rearrange("p (kt e i) -> p kt e i", kt=2 * KT, e=E)

        @block.sync
        def _(sp):
            sp.dma_start(ids_raw[:, :], ids).then_inc(ids_in, 16)
            sp.dma_start(lr_raw, low_rank.rearrange("p (a n) -> p a n", a=2)).then_inc(lr_in, 16)
            wa_raw = raw[1][:, 0:KT * WCOLS].rearrange("p (k n) -> p k n", k=KT)
            wa_dram = w_attn.rearrange("(k p) n -> p k n", p=P)
            sp.dma_start(wa_raw[:, :, 0:WQK], wa_dram[:, :, 0:WQK]).then_inc(wa_in, 16)
            sp.dma_start(gn_sb[:, :], g_norm).then_inc(gn_in, 16)
            for t in range(2):
                sp.wait_ge(gathered[t], 16)
            sp.dma_start(wa_raw[:, :, WQK:WCOLS], wa_dram[:, :, WQK:WCOLS]).then_inc(wa_rest_in, 16)
            for t in range(2):
                sp.wait_ge(gathered[t], 32)
            sp.dma_start(raw[1][:, KT * WCOLS:KT * WCOLS + H * D].rearrange("p (h n) -> p h n", h=H),
                         w_o.rearrange("(h p) n -> p h n", p=P)).then_inc(wo_in, 16)

            def of_expert(w, e, cols=slice(None)):
                if isinstance(e, int):
                    return w[e, :, cols]
                return w[bass.ds(e, 1), :, cols].rearrange("e p n -> p (e n)")

            def load_expert(e, s, refill=False):
                if refill:
                    sp.wait_ge(w13_lo_done, (e - 2) * FC + FC // 2)
                sp.dma_start(raw[s][:, 0:HALF13], of_expert(w13, e, slice(0, HALF13))).then_inc(raw13a_in[s], 16)
                if refill:
                    sp.wait_ge(w13_lo_done, (e - 1) * FC)
                sp.dma_start(raw[s][:, HALF13:W13], of_expert(w13, e, slice(HALF13, W13))).then_inc(raw13b_in[s], 16)
                if refill:
                    sp.wait_ge(w2_lo_done, (e - 1) * FC)
                sp.dma_start(raw[s][:, W13:W13 + (FC - 1) * D], of_expert(w2_main, e)).then_inc(raw2_in[s], 16)
                sp.dma_start(raw[s][0:FT, W13 + (FC - 1) * D:RAW], of_expert(w2_tail, e)).then_inc(raw2_in[s], 16)

            load_expert(0, 0)
            sp.wait_ge(wa_lo_done, 3)
            load_expert(1, 1)

            def store_h2(j):
                sp.wait_ge(h2_done, j + 1)
                sp.dma_start(scratch[:, :, bass.ds(j, 1), :].rearrange("t p j d -> p t (j d)"),
                             Hres[:, bass.ds(j * 2, 2), :]).then_inc(h2_stored, 16)

            with sp.Fori(0, NP) as j:
                store_h2(j)
            sp.wait_ge(h2_stored, 16 * NP)

            def load_residual(e, s):
                sp.dma_start(h_res[:, s, :].rearrange("p (t d) -> p t d", t=2),
                             scratch[:, bass.ds(e * POS, POS), :, :].rearrange("t i j d -> (i j) t d")
                             ).then_inc(res_in[s], 16)

            def store_out(e, s):
                sp.wait_ge(y_done, e + 1)
                sp.dma_start(of_expert(out, e), y_out[:, s, :]).then_inc(stored[s], 16)

            load_expert(2, 0, refill=True)

            sp.wait_ge(x2lo_done, NP)
            load_residual(0, 0)
            load_residual(1, 1)

            def expert(e, s):
                if not isinstance(e, int) or e + 2 < E:
                    load_expert(e + 2, s, refill=True)
                store_out(e - 1, 1 - s)
                if not isinstance(e, int) or e + 1 < E:
                    load_residual(e + 1, 1 - s)

            with sp.Fori(0, E // 2 - 2) as pair:
                for s in range(2):
                    expert(pair * 2 + (1 + s), 1 - s)
            for e in range(E - 3, E + 1):
                expert(e, e % 2)
            for s in range(2):
                sp.wait_ge(stored[s], 16 * (E // 2))

        @block.gpsimd
        def _(pool):
            def select(n, tile, op, fill, base, step, channel):
                pool.wait_ge(consts, n)
                nc.gpsimd.affine_select(out=tile, in_=tile, compare_op=op, fill=fill, base=base,
                                        pattern=[[step, P]], channel_multiplier=channel).then_inc(consts, 1)

            select(5, ident[:, :], ALU.not_equal, 1.0, 0, -1, 1)
            select(6, mask[:, :], ALU.is_ge, 0.0, 0, 1, -1)
            select(7, cum_w[0:CHUNK, :], ALU.is_ge, -1.0 / GATE_NORM, 0, 1, -1)
            select(8, cum_w[CHUNK:P, :], ALU.is_ge, 0.0, -CHUNK, 1, -1)
            pool.wait_ge(consts, 9)
            pool.wait_ge(ids_done, 3)

            def gather(j):
                if on(j):
                    for t in range(2):
                        need(pool, gathered[t], 16 * j)
                    nc.gpsimd.tensor_copy(ids_now[:, :], ids_ok[:, bass.ds(j * 2, 2)]).then_inc(ids_sel, 1)
                    need(pool, h_done, j)
                    need(pool, lt_done, j)
                    wait_apart(pool, ids_sel, j + 1, pool_passed)
                    for t in range(2):
                        nc.gpsimd.indirect_dma_start(
                            G[:, t, :], None, table,
                            bass.IndirectOffsetOnAxis(ap=ids_now[:, t:t + 1], axis=0)).then_inc(gathered[t], 16)

            def split_first(c):
                cols = first13(c)
                pool.wait_ge(w13_hi_done, c + 1)
                nc.gpsimd.tensor_tensor(e_lo[:, cols], raw[0][:, cols],
                                        e_hi[:, cols].bitcast(f32), ALU.subtract).then_inc(w13_lo_done, 1)

            def step(i):
                def second_rstd():
                    j = i - 2
                    need(pool, rstd2_done, j)
                    wait_apart(pool, mv2_done, j + 1, pool_passed)
                    nc.gpsimd.tensor_scalar(veps2[:, :], mv2[:, :, 1], 1.0, EPS, ALU.mult, ALU.add).then_inc(veps2_done, 1)
                    pool.wait_ge(veps2_done, j + 1)
                    need(pool, xn2_done, j)
                    nc.gpsimd.tensor_tensor(rstd2[:, :], veps2[:, :], minus_half[:, 0:2], ALU.pow).then_inc(rstd2_done, 1)
                if on(i - 2) and not late(i - 1):
                    second_rstd()
                if on(i + 1):
                    j = i + 1
                    need(pool, rstd_done, j)
                    wait_apart(pool, mv_done, j + 1, pool_passed)
                    nc.gpsimd.tensor_scalar(veps[:, :], mv[:, :, 1], 1.0, EPS, ALU.mult, ALU.add).then_inc(veps_done, 1)
                    pool.wait_ge(veps_done, j + 1)
                    need(pool, xn_done, j)
                    nc.gpsimd.tensor_tensor(rstd[:, :], veps[:, :], minus_half[:, 0:2], ALU.pow).then_inc(rstd_done, 1)
                    if not on(i - 1):
                        gather(j + 1)
                if on(i - 1):
                    j = i - 1
                    for t in range(2):
                        need(pool, rr_done, 2 * j + t - 1)
                        wait_apart(pool, ss_done, 2 * j + t + 1, pool_passed)
                        nc.gpsimd.tensor_scalar(ms[:, t, :], ss[:, t, :], 1.0 / DV, EPS, ALU.mult, ALU.add).then_inc(ms_done, 1)
                        pool.wait_ge(ms_done, 2 * j + t + 1)
                        need(pool, og_done, 2 * j + t - 1)
                        nc.gpsimd.tensor_tensor(rr[:, t, :], ms[:, t, :], minus_half[:, 0:H], ALU.pow).then_inc(rr_done, 1)
                    if late(j):
                        second_rstd()
                    if on(i + 1):
                        gather(i + 2)
                if first_chunk(i):
                    split_first(i - 2)

            gather(0)
            for i in (-1, 0, 1):
                step(i)
            with pool.Fori(2, NP - 2) as i:
                step(i)
            for i in (NP - 2, NP - 1, NP, NP + 1):
                step(i)

            def expert(e, s):
                for c in range(FC):
                    a, n = chunk13(c)
                    pool.wait_ge(w13_hi_done, (e + 1) * FC + c + 1)
                    nc.gpsimd.tensor_tensor(e_lo[:, a:a + n], raw[1 - s][:, a:a + n],
                                            e_hi[:, a:a + n].bitcast(f32), ALU.subtract).then_inc(w13_lo_done, 1)

            with pool.Fori(0, E // 2 - 1) as pair:
                for s in range(2):
                    expert(pair * 2 + s, s)
            expert(E - 2, 0)

        @block.scalar
        def _(act):
            def copy(dst, src):
                return nc.scalar.activation(dst, src, ACT.Copy)

            def table_set(n):
                act.add_instruction(mybir.InstLoadActFuncSet(
                    name=nc.get_next_instruction_name(), engine=mybir.EngineType.Activation, act_func_set_id=n))

            wa_raw = raw[1][:, 0:KT * WCOLS].rearrange("p (k n) -> p k n", k=KT)
            act.wait_ge(ones_done, 1)
            act.wait_ge(lr_in, 16)
            copy(lr_w[:, :, :], lr_raw).then_inc(lr_hi_done, 1)
            act.wait_ge(wa_in, 16)
            copy(wa_hi[:, :, 0:WQK], wa_raw[:, :, 0:WQK]).then_inc(wa_hi_done, 1)

            def step(i):
                en, fw, bk, cc = i + 1, i, i - 1, i - 2
                if on(fw):
                    j = fw
                    act.wait_ge(xt_done, j + 1)
                    need(act, v_done, 2 * j)
                    copy(x_hi[:, :, :].rearrange("p k n -> p (k n)"), xt_ps[:, :]).then_inc(xhi_done, 1)
                if isinstance(i, int) and i == 0:
                    act.wait_ge(wa_rest_in, 16)
                    copy(wa_hi[:, :, WQK:], wa_raw[:, :, WQK:]).then_inc(wa_hi_done, 1)
                parts = rank_parts(i)
                if parts:
                    act.wait_ge(lrx_done, i + 2)
                    need(act, lora_done, least(i + 1, NP))
                    need(act, z_done, i)
                    copy(lr_x[0:RANK, parts, :], lr_ps[:, parts, :]).then_inc(lrx_hi_done, 1)
                    act.wait_ge(lrx_hi_done, i + 2)
                    copy(lr_x[2 * BLK:2 * BLK + RANK, parts, :], lr_x[0:RANK, parts, :].bitcast(f32)).then_inc(lrx_dup_done, 1)
                if first_chunk(i):
                    c = i - 2
                    act.wait_ge(raw13a_in[0], 16)
                    act.wait_ge(raw13b_in[0], 16)
                    act.wait_ge(raw2_in[0], 32)
                    copy(e_hi[:, first13(c)], raw[0][:, first13(c)]).then_inc(w13_hi_done, 1)
                    rows, cols = first2(c)
                    copy(e_hi[rows, cols], raw[0][rows, cols]).then_inc(w2_hi_done, 1)

                def square(t):
                    j = bk
                    act.wait_ge(pv_done, 2 * j + t + 1)
                    need(act, ss_done, 2 * j + t)
                    nc.scalar.activation(sq[:, :], o_ps[t][:, :], ACT.Square).then_inc(sq_done, 1)

                def o_high(t):
                    j = bk
                    act.wait_ge(ot_done, 2 * j + t + 1)
                    need(act, wo_done, j)
                    copy(o_hi[:, t, :, :].rearrange("p h n -> p (h n)"), o_ps[t][:, :]).then_inc(ohi_done, 1)

                def v_copy(t):
                    j = fw
                    act.wait_ge(v_done, 2 * j + t + 1)
                    need(act, pv_done, 2 * j + t - 1)
                    copy(v_sb[:, t, :], v_ps[:, :]).then_inc(v_copied, 1)

                def silu(j, t):
                    act.wait_ge(g_done, 2 * j + t + 1)
                    need(act, og_done, 2 * j + t - 1)
                    nc.scalar.activation(sg[:, t, :], gate_bank(j, t)[:, :], ACT.Silu).then_inc(silu_done, 1)

                def x2_high():
                    j = cc
                    act.wait_ge(xt2_done, j + 1)
                    copy(x2_view(x2_hi, j), xt2_src()).then_inc(x2hi_done, 1)
                if on(fw):
                    table_set(TABLE_LN_EXP)
                if on(bk):
                    square(0)
                if on(cc) and not late(bk):
                    x2_high()
                if on(fw):
                    j = fw
                    act.wait_ge(z_done, j + 1)
                    need(act, gk_done, j)
                    nc.scalar.activation(lsig[:, :], z_ps[:, :], ACT.Abs).then_inc(abs_done, 1)
                    act.wait_ge(abs_done, j + 1)
                    nc.scalar.activation(lsig[:, :], lsig[:, :], ACT.Exp, scale=-1.0).then_inc(exp_done, 1)
                    act.wait_ge(exp_done, j + 1)
                    nc.scalar.activation(lsig[:, :], lsig[:, :], ACT.Ln, bias=1.0).then_inc(ln_done, 1)
                if on(bk):
                    square(1)
                    if late(bk):
                        silu(bk, 0)
                        silu(bk, 1)
                if on(fw):
                    v_copy(0)
                if on(bk):
                    o_high(0)
                if on(fw):
                    j = fw
                    act.wait_ge(cum_done, j + 1)
                    need(act, qg_done, j)
                    nc.scalar.activation(e_pos[:, :, :].rearrange("p k n -> p (k n)"), cum_ps[:, :], ACT.Exp).then_inc(epos_done, 1)
                    need(act, kg_done, j)
                    nc.scalar.activation(e_neg[:, :, :].rearrange("p k n -> p (k n)"), cum_ps[:, :], ACT.Exp, scale=-1.0).then_inc(eneg_done, 1)
                    table_set(TABLE_SILU)
                    if not late(fw):
                        silu(fw, 0)
                    v_copy(1)
                    if not late(fw):
                        silu(fw, 1)
                if on(bk):
                    o_high(1)
                if late(bk):
                    x2_high()
            for i in (-1, 0, 1):
                step(i)
            with act.Fori(2, NP - 1) as i:
                step(i)
            for i in (NP - 1, NP, NP + 1):
                step(i)

            def w13_high(e, s, c):
                a, n = chunk13(c)
                if c == 0:
                    act.wait_ge(raw13a_in[1 - s], raw_count(e + 1, 1 - s))
                if c == FC // 2:
                    act.wait_ge(raw13b_in[1 - s], raw_count(e + 1, 1 - s))
                act.wait_ge(up_done, e * FC + c + 1)
                copy(e_hi[:, a:a + n], raw[1 - s][:, a:a + n]).then_inc(w13_hi_done, 1)

            def w2_high(e, s, c):
                a, n = chunk2(c)
                if c == 0:
                    act.wait_ge(raw2_in[1 - s], raw_count(e + 1, 1 - s) * 2)
                act.wait_ge(down_done, e * FC + c + 1)
                copy(e_hi[0:rows2(c), a:a + n], raw[1 - s][0:rows2(c), a:a + n]).then_inc(w2_hi_done, 1)

            def expert(e, s, before=True, after=True):
                for c in range(FC):
                    n = e * FC + c
                    r = rows2(c)
                    act.wait_ge(up_done, n + 1)
                    need(act, mul_done, n - 2)
                    w = c % 3 * ET
                    nc.scalar.activation(s_act[0:r, w:w + ET], gu_ps[c % 3][0:r, 0:ET], ACT.Silu).then_inc(act_done, 1)
                    if after:
                        w13_high(e, s, c)
                    if c >= 2 and after:
                        w2_high(e, s, c - 2)
                    if c < 2 and before:
                        w2_high(e - 1, 1 - s, FC - 2 + c)

            expert(0, 0, before=False)
            expert(1, 1)
            with act.Fori(1, E // 2 - 1) as pair:
                for s in range(2):
                    expert(pair * 2 + s, s)
            expert(E - 2, 0)
            expert(E - 1, 1, after=False)

        @block.vector
        def _(dve):
            nc.vector.memset(ident[:, :], 0.0).then_inc(consts, 1)
            nc.vector.memset(mask[:, :], float(DK) ** -0.5).then_inc(consts, 1)
            nc.vector.memset(cum_w[0:CHUNK, :], 0.0).then_inc(consts, 1)
            nc.vector.memset(cum_w[CHUNK:P, :], 1.0 / GATE_NORM).then_inc(consts, 1)
            nc.vector.memset(minus_half[:, :], -0.5).then_inc(consts, 1)
            nc.vector.memset(lr_x[:, :, :].bitcast(f32), 1.0).then_inc(ones_done, 1)
            dve.wait_ge(ids_in, 16)
            nc.vector.tensor_scalar(ids_f[:, :], ids_raw[:, :], 0.0, float(VOCAB), ALU.is_lt, ALU.mult).then_inc(ids_done, 1)
            dve.wait_ge(ids_done, 1)
            nc.vector.tensor_tensor(ids_f[:, :], ids_raw[:, :], ids_f[:, :], ALU.add).then_inc(ids_done, 1)
            dve.wait_ge(ids_done, 2)
            nc.vector.tensor_scalar(ids_ok[:, :], ids_f[:, :], 0.0, float(VOCAB - 1), ALU.max, ALU.min).then_inc(ids_done, 1)

            wa_raw = raw[1][:, 0:KT * WCOLS].rearrange("p (k n) -> p k n", k=KT)
            wo_raw = raw[1][:, KT * WCOLS:KT * WCOLS + H * D]
            wo_hi2 = wo_hi[:, :, :].rearrange("p h n -> p (h n)")
            wo_lo2 = wo_lo[:, :, :].rearrange("p h n -> p (h n)")
            wo_scaled, wo_hi_done = sem("wo_scaled"), sem("wo_hi_done")

            def wa_low(part, cols):
                dve.wait_ge(wa_hi_done, part)
                nc.vector.tensor_tensor(wa_lo[:, :, cols], wa_raw[:, :, cols],
                                        wa_hi[:, :, cols].bitcast(f32), ALU.subtract).then_inc(wa_lo_done, 1)

            dve.wait_ge(lr_hi_done, 1)
            nc.vector.tensor_tensor(lr_w[2 * BLK:, :, :], lr_raw[2 * BLK:, :, :],
                                    lr_w[2 * BLK:, :, :].bitcast(f32), ALU.subtract).then_inc(lr_lo_done, 1)
            wa_low(1, slice(0, WQK))

            def norm(src, j, stats, mv, bn_done, mv_done, rstd_done, xn_done):
                for t in range(2):
                    last = nc.vector.bn_stats(stats[:, t, :], src[:, bass.ds(2 * j + t, 1), :].rearrange("p o d -> p (o d)"))
                last.then_inc(bn_done, 1)
                need(dve, rstd_done, j)
                need(dve, xn_done, j)
                wait_apart(dve, bn_done, j + 1, dve_passed)
                for t in range(2):
                    last = nc.vector.bn_aggr(mv[:, t, :], stats[:, t, :])
                last.then_inc(mv_done, 1)

            def normed(dst, src, j, mv, rstd, xn_done):
                for t in range(2):
                    last = nc.vector.tensor_scalar(
                        dst[:, t, :], src[:, bass.ds(2 * j + t, 1), :].rearrange("p o d -> p (o d)"),
                        mv[:, t, 0:1], rstd[:, t:t + 1], ALU.subtract, ALU.mult)
                last.then_inc(xn_done, 1)

            def step(i):
                en, fw, bk, cc = i + 1, i, i - 1, i - 2

                def mask_scores():
                    j = bk
                    dve.wait_ge(a_done, j + 1)
                    dve.wait_ge(consts, 9)
                    need(dve, pv_done, 2 * j)
                    for r in range(2):
                        nc.vector.tensor_tensor(
                            am[:, r, :, :, :].rearrange("p a b t -> p (a b) t"),
                            a_ps[r][:, :].rearrange("p (n t) -> p n t", t=P),
                            mask[:, :].unsqueeze(1).broadcast_to([P, 4, P]), ALU.mult).then_inc(am_done, 1)

                if on(fw):
                    dve.wait_ge(xhi_done, fw + 1)
                    nc.vector.tensor_tensor(x_lo[:, :, :].rearrange("p k n -> p (k n)"), xt_ps[:, :],
                                            x_hi[:, :, :].rearrange("p k n -> p (k n)").bitcast(f32),
                                            ALU.subtract).then_inc(xlo_done, 1)
                if isinstance(i, int) and i == 0:
                    wa_low(2, slice(WQK, WCOLS))
                if on(bk):
                    mask_scores()

                def second_normed():
                    j = cc
                    dve.wait_ge(rstd2_done, j + 1)
                    need(dve, xt2_done, j)
                    normed(xn2, Hres, j, mv2, rstd2, xn2_done)
                if on(cc):
                    j = cc
                    dve.wait_ge(wo_done, j + 1)
                    rows = Hres[:, bass.ds(2 * j, 2), :]
                    nc.vector.tensor_tensor(rows, rows, wo_ps[:, :].rearrange("p (t d) -> p t d", t=2), ALU.add).then_inc(h2_done, 1)
                    need(dve, mv2_done, j)
                    wait_apart(dve, h2_done, j + 1, dve_passed)
                    norm(Hres, j, stats2, mv2, bn2_done, mv2_done, rstd2_done, xn2_done)
                parts = rank_parts(i)
                if parts:
                    dve.wait_ge(lrx_hi_done, i + 2)
                    nc.vector.tensor_tensor(lr_x[BLK:BLK + RANK, parts, :], lr_ps[:, parts, :],
                                            lr_x[0:RANK, parts, :].bitcast(f32), ALU.subtract).then_inc(lrx_lo_done, 1)
                if on(cc) and not late(bk):
                    second_normed()
                if on(en):
                    j = en
                    dve.wait_ge(lora_done, j + 1)
                    for t in range(2):
                        dve.wait_ge(gathered[t], 16 * j + 16)
                    nc.vector.tensor_tensor(Hres[:, bass.ds(2 * j, 2), :], G[:, :, 0:D],
                                            lora_ps[:, :].rearrange("p (t d) -> p t d", t=2), ALU.add).then_inc(h_done, 1)
                    need(dve, mv_done, j)
                    wait_apart(dve, h_done, j + 1, dve_passed)
                    norm(Hres, j, stats, mv, bn_done, mv_done, rstd_done, xn_done)
                def sums(t):
                    j = bk
                    dve.wait_ge(sq_done, 2 * j + t + 1)
                    need(dve, ms_done, 2 * j + t - 1)
                    nc.vector.tensor_reduce(ss[:, t, :], sq[:, :].rearrange("p (h n) -> p h n", h=H), AX.X,
                                            ALU.add).then_inc(ss_done, 1)

                def gated(t):
                    j = bk
                    dve.wait_ge(rr_done, 2 * j + t + 1)
                    dve.wait_ge(silu_done, 2 * j + t + 1)
                    need(dve, ot_done, 2 * j + t - 1)
                    for h in range(H):
                        cols = slice(h * DV, (h + 1) * DV)
                        last = nc.vector.scalar_tensor_tensor(og[:, t, cols], o_ps[t][:, cols], rr[:, t, h:h + 1],
                                                              sg[:, t, cols], ALU.mult, ALU.mult)
                    last.then_inc(og_done, 1)

                def o_low(t):
                    j = bk
                    dve.wait_ge(ohi_done, 2 * j + t + 1)
                    nc.vector.tensor_tensor(o_lo[:, t, :, :].rearrange("p h n -> p (h n)"), o_ps[t][:, :],
                                            o_hi[:, t, :, :].rearrange("p h n -> p (h n)").bitcast(f32),
                                            ALU.subtract).then_inc(olo_done, 1)

                def x2_low():
                    j = cc
                    dve.wait_ge(x2hi_done, j + 1)
                    nc.vector.tensor_tensor(x2_view(x2_lo, j), xt2_src(), x2_view(x2_hi, j).bitcast(f32),
                                            ALU.subtract).then_inc(x2lo_done, 1)
                if on(bk):
                    sums(0)
                if on(cc) and not late(bk):
                    x2_low()
                if on(fw):
                    j = fw
                    dve.wait_ge(ln_done, j + 1)
                    need(dve, cum_done, j)
                    nc.vector.scalar_tensor_tensor(gk[:, :, :].rearrange("p a b -> p (a b)"), z_ps[:, :], 0.0,
                                                   lsig[:, :], ALU.min, ALU.subtract).then_inc(gk_done, 1)
                if on(bk):
                    if late(bk):
                        sums(1)
                    gated(0)
                    if not late(bk):
                        sums(1)
                if on(en):
                    j = en
                    dve.wait_ge(rstd_done, j + 1)
                    need(dve, xt_done, j)
                    normed(xn, Hres, j, mv, rstd, xn_done)
                if on(bk):
                    if late(bk):
                        gated(1)
                        o_low(0)
                    else:
                        o_low(0)
                        gated(1)
                if on(fw):
                    j = fw
                    dve.wait_ge(epos_done, j + 1)
                    dve.wait_ge(q_done, j + 1)
                    need(dve, a_done, j)
                    nc.vector.tensor_tensor(qg[:, :, :].rearrange("p k n -> p (k n)"), q_ps[:, :],
                                            e_pos[:, :, :].rearrange("p k n -> p (k n)"), ALU.mult).then_inc(qg_done, 1)
                    dve.wait_ge(eneg_done, j + 1)
                    dve.wait_ge(k_done, j + 1)
                    nc.vector.tensor_tensor(kg[:, :, :].rearrange("p k n -> p (k n)"), k_ps[:, :],
                                            e_neg[:, :, :].rearrange("p k n -> p (k n)"), ALU.mult).then_inc(kg_done, 1)
                if on(bk):
                    o_low(1)
                    if late(bk):
                        second_normed()
                        x2_low()
                if first_chunk(i):
                    c = i - 2
                    rows, cols = first2(c)
                    dve.wait_ge(w2_hi_done, c + 1)
                    nc.vector.tensor_tensor(e_lo[rows, cols], raw[0][rows, cols], e_hi[rows, cols].bitcast(f32),
                                            ALU.subtract).then_inc(w2_lo_done, 1)
                if isinstance(i, int) and i == 0:
                    dve.wait_ge(wo_in, 16)
                    dve.wait_ge(gn_in, 16)
                    nc.vector.tensor_scalar(wo_raw, wo_raw, gn_sb[:, 0:1], None, ALU.mult).then_inc(wo_scaled, 1)
                    dve.wait_ge(wo_scaled, 1)
                    nc.vector.tensor_copy(wo_hi2, wo_raw).then_inc(wo_hi_done, 1)
                    dve.wait_ge(wo_hi_done, 1)
                    nc.vector.tensor_tensor(wo_lo2, wo_raw, wo_hi2.bitcast(f32), ALU.subtract).then_inc(wa_lo_done, 1)

            for i in (-1, 0, 1):
                step(i)
            with dve.Fori(2, NP - 1) as i:
                step(i)
            for i in (NP - 1, NP, NP + 1):
                step(i)

            def w2_low(e, s, c):
                a, n = chunk2(c)
                r = rows2(c)
                dve.wait_ge(w2_hi_done, (e + 1) * FC + c + 1)
                nc.vector.tensor_tensor(e_lo[0:r, a:a + n], raw[1 - s][0:r, a:a + n],
                                        e_hi[0:r, a:a + n].bitcast(f32), ALU.subtract).then_inc(w2_lo_done, 1)

            def result(e, s):
                dve.wait_ge(down_done, (e + 1) * FC)
                dve.wait_ge(res_in[s], (e // 2 + 1) * 16 if isinstance(e, int) else (e - s) * 8 + 16)
                need(dve, stored[s], (e // 2) * 16 if isinstance(e, int) else (e - s) * 8)
                for t in range(2):
                    last = nc.vector.tensor_tensor(y_out[:, s, t * D:(t + 1) * D], y_ps[t][:, 0:D],
                                                   h_res[:, s, t * D:(t + 1) * D], ALU.add)
                last.then_inc(y_done, 1)

            def expert(e, s, before=True, after=True):
                for c in range(FC):
                    n = e * FC + c
                    r = rows2(c)
                    w = c % 3 * ET
                    if c == 1 and before:
                        result(e - 1, 1 - s)
                    dve.wait_ge(act_done, n + 1)
                    need(dve, hlo_done, n - 2)
                    up = gu_ps[c % 3][:, ET:2 * ET] if r == P else gu_ps[c % 3][FT:2 * FT, 0:ET]
                    nc.vector.tensor_tensor(h32[0:r, w:w + ET], s_act[0:r, w:w + ET], up, ALU.mult).then_inc(mul_done, 1)
                    dve.wait_ge(mul_done, n + 1)
                    need(dve, down_done, n - 2)
                    nc.vector.tensor_copy(h_hi[0:r, w:w + ET], h32[0:r, w:w + ET]).then_inc(hhi_done, 1)
                    dve.wait_ge(hhi_done, n + 1)
                    nc.vector.tensor_tensor(h_lo[0:r, w:w + ET], h32[0:r, w:w + ET],
                                            h_hi[0:r, w:w + ET].bitcast(f32), ALU.subtract).then_inc(hlo_done, 1)
                    if c >= 2 and after:
                        w2_low(e, s, c - 2)
                    if c < 2 and before:
                        w2_low(e - 1, 1 - s, FC - 2 + c)

            expert(0, 0, before=False)
            expert(1, 1)
            with dve.Fori(1, E // 2 - 1) as pair:
                for s in range(2):
                    expert(pair * 2 + s, s)
            expert(E - 2, 0)
            expert(E - 1, 1, after=False)
            result(E - 1, 1)

        @block.tensor
        def _(pe):
            mm = nc.tensor.matmul

            def split_mm(out, w_pairs, x_pairs):
                n = len(w_pairs)
                for k, ((wh, wl), (xh, xl)) in enumerate(zip(w_pairs, x_pairs)):
                    mm(out, wh, xh, start=k == 0, stop=False)
                    mm(out, wh, xl, start=False, stop=False)
                    last = mm(out, wl, xh, start=False, stop=k == n - 1)
                return last

            COL_Q, COL_K, COL_G, COL_V = RANK, RANK + D, RANK + 2 * D, RANK + 2 * D + NV

            def weights(c0, n):
                return [(wa_hi[:, k, c0:c0 + n], wa_lo[:, k, c0:c0 + n]) for k in range(KT)]

            def tokens(c0, n):
                return [(x_hi[:, k, c0:c0 + n], x_lo[:, k, c0:c0 + n]) for k in range(KT)]

            pe.wait_ge(consts, 9)

            def step(i):
                en, fw, bk, cc = i + 1, i, i - 1, i - 2
                if on(fw):
                    j = fw
                    pe.wait_ge(xn_done, j + 1)
                    need(pe, olo_done, 2 * j - 3)
                    for t in range(2):
                        for k in range(KT):
                            last = nc.tensor.transpose(xt_ps[:, k * PT + t * S:k * PT + (t + 1) * S],
                                                       xn[:, t, k * P:(k + 1) * P], ident[:, :])
                    last.then_inc(xt_done, 1)
                def output_projection(j, t):
                    if isinstance(j, int) and j == 0:
                        pe.wait_ge(wa_lo_done, 3)
                    need(pe, silu_done, min(2 * j + 3, 2 * NP - 2 + 2 * late(j)) if isinstance(j, int) else 2 * j + 3)
                    pe.wait_ge(olo_done, 2 * j + t + 1)
                    return split_mm(wo_ps[:, t * D:(t + 1) * D],
                                    [(o_hi[:, t, h, :], o_lo[:, t, h, :]) for h in range(H)],
                                    [(wo_hi[:, h, :], wo_lo[:, h, :]) for h in range(H)])

                def lora():
                    j = en
                    if isinstance(j, int) and j == 0:
                        pe.wait_ge(lr_lo_done, 1)
                    pe.wait_ge(lrx_dup_done, i + 2)
                    pe.wait_ge(lrx_lo_done, i + 2)
                    need(pe, h2_done, j - 2)
                    for t in range(2):
                        last = mm(lora_ps[:, t * D:(t + 1) * D], lr_x[0:LK, 0, t * S:(t + 1) * S], lr_w[0:LK, 0, :],
                                  start=True, stop=True)
                    last.then_inc(lora_done, 1)

                if on(cc):
                    output_projection(cc, 0)
                if on(bk):
                    j = bk
                    pe.wait_ge(kg_done, j + 1)
                    pe.wait_ge(v_copied, 2 * j + 2)
                    for t in range(2):
                        for m in range(2):
                            for r in range(2):
                                rows = slice(r * DK, (r + 1) * DK)
                                cols = slice((t * 2 + m) * P, (t * 2 + m + 1) * P)
                                last = mm(a_ps[r][:, cols], kg[rows, m, t * S:(t + 1) * S],
                                          qg[rows, m, t * S:(t + 1) * S], start=True, stop=True)
                    last.then_inc(a_done, 1)
                def xt2(j):
                    pe.wait_ge(xn2_done, j + 1)
                    pe.wait_ge(lrx_lo_done, least(j + 4, NP + 1))
                    need(pe, x2lo_done, j)
                    for t in range(2):
                        for k in range(KT):
                            last = nc.tensor.transpose(xt2_ps[:, k * PT + t * S:k * PT + (t + 1) * S],
                                                       xn2[:, t, k * P:(k + 1) * P], ident[:, :])
                    last.then_inc(xt2_done, 1)
                if late(cc):
                    xt2(cc - 1)
                if on(cc):
                    output_projection(cc, 1).then_inc(wo_done, 1)
                if on(en):
                    j = en
                    for t in range(2):
                        pe.wait_ge(gathered[t], 16 * j + 16)
                    need(pe, silu_done, 2 * i)
                    need(pe, lrx_lo_done, i + 1)
                    for t in range(2):
                        last = nc.tensor.transpose(lr_ps[:, 0, t * S:(t + 1) * S], G[:, t, D:TW], ident[:, :])
                    last.then_inc(lt_done, 1)
                    if not on(fw):
                        pe.wait_ge(lt_done, j + 1)
                        pe.sem_inc(lrx_done, 1)
                if on(fw):
                    j = fw
                    pe.wait_ge(xlo_done, j + 1)
                    if isinstance(j, int) and j == 0:
                        pe.wait_ge(wa_lo_done, 1)
                    need(pe, silu_done, 2 * j)
                    split_mm(lr_ps[:, 1, :], weights(0, RANK), tokens(0, PT)).then_inc(lrx_done, 1)
                if on(fw):
                    j = fw
                    need(pe, qg_done, j)
                    for m in range(KT):
                        last = split_mm(q_ps[:, m * PT:(m + 1) * PT], weights(COL_Q + m * P, P), tokens(0, PT))
                    last.then_inc(q_done, 1)
                if on(fw):
                    j = fw
                    need(pe, kg_done, j)
                    for m in range(KT):
                        last = split_mm(k_ps[:, m * PT:(m + 1) * PT], weights(COL_K + m * P, P), tokens(0, PT))
                    last.then_inc(k_done, 1)
                if on(en):
                    lora()

                def values(t):
                    j = bk
                    pe.wait_ge(am_done, 2 * j + 2)
                    if t == 0:
                        need(pe, xlo_done, least(j + 2, NP))
                        need(pe, olo_done, 2 * j - 1)
                    else:
                        need(pe, olo_done, 2 * j)
                    for h in range(H):
                        last = mm(o_ps[t][:, h * DV:(h + 1) * DV], am[:, h % 2, t, h // 2, :],
                                  v_sb[:, t, h * DV:(h + 1) * DV], start=True, stop=True)
                    last.then_inc(pv_done, 1)

                def output_gate(j, t):
                    if isinstance(j, int) and j == 0:
                        pe.wait_ge(wa_lo_done, 2)
                    if late(j):
                        pe.wait_ge(kg_done, NP)
                    elif t == 0:
                        need(pe, h_done, least(j + 2, NP))
                        need(pe, h2_done, j - 1)
                    else:
                        pe.wait_ge(lrx_lo_done, j + 2)
                        need(pe, x2lo_done, j - 1)
                    split_mm(gate_bank(j, t)[:, :], tokens(t * S, S), weights(COL_G, NV)).then_inc(g_done, 1)

                def v_proj(t):
                    j = fw
                    if t == 0:
                        need(pe, am_done, 2 * j)
                    else:
                        pe.wait_ge(v_copied, 2 * j + 1)
                    split_mm(v_ps[:, :], tokens(t * S, S), weights(COL_V, NV)).then_inc(v_done, 1)

                def o_transpose(t):
                    j = bk
                    pe.wait_ge(og_done, 2 * j + t + 1)
                    for h in range(H):
                        last = nc.tensor.transpose(o_ps[t][:, h * P:(h + 1) * P], og[:, t, h * DV:(h + 1) * DV], ident[:, :])
                    last.then_inc(ot_done, 1)

                if on(bk):
                    values(0)
                if on(cc) and not late(bk):
                    xt2(cc)
                if on(fw):
                    j = fw
                    pe.wait_ge(lrx_dup_done, i + 2)
                    pe.wait_ge(lrx_lo_done, i + 2)
                    need(pe, am_done, 2 * j - 1)
                    for t in range(2):
                        last = mm(z_ps[:, t * D:(t + 1) * D], lr_x[0:LK, 1, t * S:(t + 1) * S], lr_w[0:LK, 1, :],
                                  start=True, stop=True)
                    last.then_inc(z_done, 1)
                    if not late(fw):
                        output_gate(j, 0)
                if on(bk):
                    values(1)
                if late(bk):
                    output_gate(bk, 0)
                    output_gate(bk, 1)
                if on(fw):
                    v_proj(0)
                if on(fw):
                    j = fw
                    pe.wait_ge(gk_done, j + 1)
                    for t in range(2):
                        for m in range(KT):
                            last = mm(cum_ps[:, m * PT + t * S:m * PT + (t + 1) * S], gk[:, t, m * P:(m + 1) * P],
                                      cum_w[:, :], start=True, stop=True)
                    last.then_inc(cum_done, 1)
                if on(bk):
                    o_transpose(0)
                if on(fw):
                    v_proj(1)
                    if not late(fw):
                        output_gate(fw, 1)
                if on(bk):
                    o_transpose(1)

            steps(pe, step)

            pe.wait_ge(x2lo_done, NP)

            def up(e, c):
                n = e * FC + c
                pe.wait_ge(w13_lo_done, n + 1)
                need(pe, mul_done, n - 2)
                a, _ = chunk13(c)
                xs = [(x2_hi[:, bass.ds(e * KT * ET + k * ET, ET)], x2_lo[:, bass.ds(e * KT * ET + k * ET, ET)])
                      for k in range(KT)]
                parts = 2 if c < FC - 1 else 1
                width = 2 * P // parts if c < FC - 1 else 2 * FT
                width = P
                for g in range(parts):
                    at = [a + k * parts * P + g * P for k in range(KT)]
                    last = split_mm(gu_ps[c % 3][:, g * ET:(g + 1) * ET],
                                    [(e_hi[:, o:o + width], e_lo[:, o:o + width]) for o in at], xs)
                last.then_inc(up_done, 1)

            def down(e, c):
                n = e * FC + c
                r = rows2(c)
                a, _ = chunk2(c)
                pe.wait_ge(hlo_done, n + 1)
                pe.wait_ge(w2_lo_done, n + 1)
                if c == 0:
                    need(pe, y_done, e)
                for t in range(2):
                    w = c % 3 * ET + t * P
                    hh, hl = h_hi[0:r, w:w + P], h_lo[0:r, w:w + P]
                    wh, wl = e_hi[0:r, a:a + D], e_lo[0:r, a:a + D]
                    mm(y_ps[t][:, 0:D], hh, wh, start=c == 0, stop=False)
                    mm(y_ps[t][:, 0:D], hh, wl, start=False, stop=False)
                    last = mm(y_ps[t][:, 0:D], hl, wh, start=False, stop=c == FC - 1)
                last.then_inc(down_done, 1)

            def expert(e, s, before=True):
                for c in range(FC):
                    up(e, c)
                    if c >= 2:
                        down(e, c - 2)
                    elif before:
                        down(e - 1, FC - 2 + c)

            expert(0, 0, before=False)
            expert(1, 1)
            with pe.Fori(1, E // 2) as pair:
                for s in range(2):
                    expert(pair * 2 + s, s)
            down(E - 1, FC - 2)
            down(E - 1, FC - 1)


def kernel(x, L0_tok_base_weight, L0_tok_lora_A, L0_tok_lora_B, L0_attn_Wq, L0_attn_Wk, L0_attn_Wv,
           L0_attn_Wg, L0_attn_gk_w1, L0_attn_gk_w2, L0_attn_gk_b2, L0_attn_g_norm_w, L0_attn_Wo,
           L0_ffn_w1, L0_ffn_w3, L0_ffn_w2):
    import numpy as np
    import concourse.bacc as bacc
    from concourse.bass_utils import run_bass_kernel_spmd

    def a(v):
        return np.asarray(v)

    def chunks(w):
        w = a(w).reshape(E, KT, P, F)
        full = w[:, :, :, :(FC - 1) * P].reshape(E, KT, P, FC - 1, P).transpose(0, 2, 3, 1, 4)
        return full, w[:, :, :, (FC - 1) * P:].transpose(0, 2, 1, 3)

    (f1, t1), (f3, t3) = chunks(L0_ffn_w1), chunks(L0_ffn_w3)
    w13 = np.concatenate([np.stack([f1, f3], 4).reshape(E, P, -1), np.stack([t1, t3], 3).reshape(E, P, -1)], 2)
    w2 = a(L0_ffn_w2)
    low_rank = np.zeros((3, BLK, 2, D), a(L0_tok_lora_B).dtype)
    low_rank[:, :RANK, 0] = a(L0_tok_lora_B)
    low_rank[:, :RANK, 1] = a(L0_attn_gk_w2)
    low_rank[0::2, RANK, 1] = a(L0_attn_gk_b2)
    low_rank = low_rank.reshape(3 * BLK, 2 * D)
    arrays = {
        "ids": a(x).T,
        "table": np.concatenate([a(L0_tok_base_weight).T, a(L0_tok_lora_A)], 1),
        "w_attn": np.concatenate([a(L0_attn_gk_w1), a(L0_attn_Wq), a(L0_attn_Wk), a(L0_attn_Wg), a(L0_attn_Wv)], 1),
        "w_o": a(L0_attn_Wo),
        "low_rank": low_rank,
        "g_norm": a(L0_attn_g_norm_w)[:, None],
        "w13": w13,
        "w2_main": w2[:, :(FC - 1) * P].reshape(E, FC - 1, P, D).transpose(0, 2, 1, 3).reshape(E, P, -1),
        "w2_tail": w2[:, (FC - 1) * P:],
    }
    arrays = {k: np.ascontiguousarray(v) for k, v in arrays.items()}
    nc = bacc.Bacc("TRN2", target_bir_lowering=False, num_devices=1)
    args = [nc.dram_tensor(k, v.shape, mybir.dt.from_np(v.dtype), kind="ExternalInput").ap() for k, v in arrays.items()]
    scratch = nc.dram_tensor("scratch", [2, S, B // 2, D], mybir.dt.float32, kind="Internal").ap()
    out = nc.dram_tensor("out", [E, P, 2 * D], mybir.dt.float32, kind="ExternalOutput").ap()
    layer_kernel(nc, *args, scratch, out)
    r = run_bass_kernel_spmd(nc, [arrays], core_ids=[0])
    y = r.results[0]["out"].reshape(E, POS, B // 2, 2, D)
    return np.ascontiguousarray(y.transpose(2, 3, 0, 1, 4)).reshape(B, S, D)
```

```python
import concourse.bass as bass
from concourse import mybir
from contextlib import ExitStack


B, S, D = 16, 128, 256
VOCAB, RANK = 8000, 16
H, DV, CHUNK = 4, 128, 64
DK = D // H
NV = H * DV
GATE_NORM, EPS = 16.0, 1e-5
E, F = 8, 704
P = 128
KT = D // P
TW = D + RANK
NP = B // 2
PT = 2 * S
FC = -(-F // P)
FT = F - (FC - 1) * P
POS = S // E
ET = B * POS
WCOLS = RANK + 2 * D + 2 * NV
WQK = RANK + 2 * D
C13 = KT * 2 * P
T13 = KT * 2 * FT
W13 = (FC - 1) * C13 + T13
HALF13 = FC // 2 * C13
RAW = W13 + FC * D
BLK = 32
LK = 2 * BLK + RANK + 1
TABLE_LN_EXP, TABLE_SILU = 6, 18


def need(eng, sem, count):
    if isinstance(count, int) and count <= 0:
        return
    eng.wait_ge(sem, count)


def wait_apart(eng, sem, count, passed):
    need(eng, sem, count)
    eng.sem_inc(passed, 1)


def least(count, top):
    return min(count, top) if isinstance(count, int) else count


def layer_kernel(nc, ids, table, w_attn, w_o, low_rank, g_norm, w13, w2_main, w2_tail,
                 scratch, out):
    f32, f32r, i32 = mybir.dt.float32, mybir.dt.float32r, mybir.dt.int32
    ALU, ACT, AX = mybir.AluOpType, mybir.ActivationFunctionType, mybir.AxisListType

    ctx = ExitStack()
    with ctx:
        def sb(name, shape, dt=f32):
            return ctx.enter_context(nc.sbuf_tensor(name, shape, dt))

        def sem(name):
            return ctx.enter_context(nc.semaphore(name))

        ident = sb("ident", [P, P])
        mask = sb("mask", [P, P])
        cum_w = sb("cum_w", [P, P])
        minus_half = sb("minus_half", [P, 8])
        lr_w = sb("lr_w", [3 * BLK, 2, D], f32r)
        gn_sb = sb("gn_sb", [P, 1])
        wa_hi = sb("wa_hi", [P, KT, WCOLS], f32r)
        wa_lo = sb("wa_lo", [P, KT, WCOLS], f32r)
        wo_hi = sb("wo_hi", [P, H, D], f32r)
        wo_lo = sb("wo_lo", [P, H, D], f32r)
        raw = [sb(f"raw{s}", [P, RAW]) for s in range(2)]
        e_hi = sb("e_hi", [P, RAW], f32r)
        e_lo = sb("e_lo", [P, RAW], f32r)
        ids_raw = sb("ids_raw", [P, B], i32)
        ids_f = sb("ids_f", [P, B])
        ids_ok = sb("ids_ok", [P, B], i32)
        ids_now = sb("ids_now", [P, 2], i32)
        G = sb("G", [P, 2, TW])
        Hres = sb("Hres", [P, B, D])
        stats = sb("stats", [P, 2, 6])
        mv = sb("mv", [P, 2, 2])
        veps = sb("veps", [P, 2])
        rstd = sb("rstd", [P, 2])
        stats2 = sb("stats2", [P, 2, 6])
        mv2 = sb("mv2", [P, 2, 2])
        veps2 = sb("veps2", [P, 2])
        rstd2 = sb("rstd2", [P, 2])
        xn = sb("xn", [P, 2, D])
        x_hi = sb("x_hi", [P, KT, PT], f32r)
        x_lo = sb("x_lo", [P, KT, PT], f32r)
        lr_x = sb("lr_x", [3 * BLK, 2, PT], f32r)
        v_sb = sb("v_sb", [P, 2, NV])
        sg = sb("sg", [P, 2, NV])
        lsig = sb("lsig", [P, 2 * D])
        gk = sb("gk", [P, 2, D])
        e_pos = sb("e_pos", [P, KT, PT])
        e_neg = sb("e_neg", [P, KT, PT])
        qg = sb("qg", [P, KT, PT])
        kg = sb("kg", [P, KT, PT])
        am = sb("am", [P, 2, 2, 2, P])
        sq = sb("sq", [P, NV])
        ss = sb("ss", [P, 2, H])
        ms = sb("ms", [P, 2, H])
        rr = sb("rr", [P, 2, H])
        og = sb("og", [P, 2, NV])
        o_hi = sb("o_hi", [P, 2, H, P], f32r)
        o_lo = sb("o_lo", [P, 2, H, P], f32r)
        xn2 = sb("xn2", [P, 2, D])
        x2_hi = sb("x2_hi", [P, E * KT * ET], f32r)
        x2_lo = sb("x2_lo", [P, E * KT * ET], f32r)

        s_act = am[:, :, :, :, :].rearrange("p a b c t -> p (a b c t)")
        h32 = og[:, :, :].rearrange("p a n -> p (a n)")
        h_hi = o_hi[:, :, :, :].rearrange("p a h t -> p (a h t)")
        h_lo = o_lo[:, :, :, :].rearrange("p a h t -> p (a h t)")
        lr_raw = sq[0:3 * BLK, :].rearrange("p (a n) -> p a n", a=2)
        open_G = og[:, :, 0:TW]
        y_out, h_res = v_sb, sg

        def lr_in_bank(b):
            return b[0:RANK, :].rearrange("p (a n) -> p a n", a=2)

        bank = [ctx.enter_context(nc.psum_tensor(f"bank{n}", [P, 512], f32)) for n in range(8)]
        q_ps, k_ps = bank[0], bank[1]
        xt_ps, xt2_ps = bank[3], bank[6]
        o_ps = [bank[3], bank[2]]
        a_ps = [bank[4], bank[5]]
        z_ps = cum_ps = bank[4]
        v_ps = bank[5]
        lr_ps = lr_in_bank(bank[6])
        lora_ps = wo_ps = bank[7]
        g_ps = [bank[7], bank[6]]
        gu_ps = [bank[0], bank[1], bank[2]]
        y_ps = [bank[3], bank[4]]

        ids_in, ids_done, consts, lr_in, wa_in, wa_rest_in, wo_in, gn_in = map(
            sem, ["ids_in", "ids_done", "consts", "lr_in", "wa_in", "wa_rest_in", "wo_in", "gn_in"])
        ids_sel = sem("ids_sel")
        gathered = [sem(f"gathered{t}") for t in range(2)]
        open_gathered = [sem(f"open_gathered{t}") for t in range(2)]
        wa_hi_done, wa_lo_done, ones_done = sem("wa_hi_done"), sem("wa_lo_done"), sem("ones_done")
        lr_hi_done, lr_lo_done = sem("lr_hi_done"), sem("lr_lo_done")
        lrx_done, lrx_hi_done, lrx_dup_done, lrx_lo_done = (
            sem("lrx_done"), sem("lrx_hi_done"), sem("lrx_dup_done"), sem("lrx_lo_done"))
        lora_done, h_done = sem("lora_done"), sem("h_done")
        bn_done, mv_done, veps_done, rstd_done, xn_done = (
            sem("bn_done"), sem("mv_done"), sem("veps_done"), sem("rstd_done"), sem("xn_done"))
        xt_done, xhi_done, xlo_done = sem("xt_done"), sem("xhi_done"), sem("xlo_done")
        z_done = sem("z_done")
        abs_done, exp_done, ln_done, gk_done = sem("abs_done"), sem("exp_done"), sem("ln_done"), sem("gk_done")
        cum_done, epos_done, eneg_done = sem("cum_done"), sem("epos_done"), sem("eneg_done")
        q_done, k_done, qg_done, kg_done = sem("q_done"), sem("k_done"), sem("qg_done"), sem("kg_done")
        v_done, v_copied, g_done, silu_done = sem("v_done"), sem("v_copied"), sem("g_done"), sem("silu_done")
        a_done, am_done, pv_done = sem("a_done"), sem("am_done"), sem("pv_done")
        sq_done, ss_done, ms_done, rr_done = sem("sq_done"), sem("ss_done"), sem("ms_done"), sem("rr_done")
        og_done, ot_done, ohi_done, olo_done = sem("og_done"), sem("ot_done"), sem("ohi_done"), sem("olo_done")
        wo_done, h2_done, h2_stored = sem("wo_done"), sem("h2_done"), sem("h2_stored")
        bn2_done, mv2_done, veps2_done, rstd2_done, xn2_done = (
            sem("bn2_done"), sem("mv2_done"), sem("veps2_done"), sem("rstd2_done"), sem("xn2_done"))
        xt2_done, x2hi_done, x2lo_done = sem("xt2_done"), sem("x2hi_done"), sem("x2lo_done")
        raw13a_in, raw13b_in, raw2_in = (
            [sem(f"{part}_in{s}") for s in range(2)] for part in ("raw13a", "raw13b", "raw2"))
        w13_hi_done, w13_lo_done = sem("w13_hi_done"), sem("w13_lo_done")
        w2_hi_done, w2_lo_done = sem("w2_hi_done"), sem("w2_lo_done")
        up_done, act_done, mul_done, hhi_done, hlo_done, down_done = (
            sem("up_done"), sem("act_done"), sem("mul_done"), sem("hhi_done"), sem("hlo_done"), sem("down_done"))
        res_in = [sem(f"res_in{s}") for s in range(2)]
        y_done = sem("y_done")
        stored = [sem(f"stored{s}") for s in range(2)]

        opening = {name: sem(f"opening_{name}") for name in
                   ("lrx", "lrx_hi", "lrx_dup", "lrx_lo", "lora", "h", "bn", "mv", "veps", "rstd", "xn", "xt", "xhi")}
        closing = {name: sem(f"closing_{name}") for name in
                   ("wo", "h2", "bn2", "mv2", "veps2", "rstd2", "xn2", "xt2", "x2hi")}

        dve_passed, pool_passed = sem("dve_passed"), sem("pool_passed")

        block = ctx.enter_context(nc.Block())

        open_lr, open_lora, open_xt = [bank[6], bank[4]], [bank[7], bank[5]], [bank[3], bank[2]]
        close_wo, close_xt2 = [bank[7], bank[5]], [bank[6], bank[4]]

        def steps(eng, step):
            for i in (0, 1):
                step(i)
            with eng.Fori(2, NP - 1) as i:
                step(i)
            for i in (NP - 1, NP):
                step(i)

        def on(j):
            return not isinstance(j, int) or 0 <= j < NP

        def opened(j):
            return isinstance(j, int) and j == 0

        def late(j):
            return isinstance(j, int) and j == NP - 1

        def gate_bank(j, t):
            return bank[t] if late(j) else g_ps[t]

        def of(t, first, pair):
            return pair if t else first

        def rank_parts(i):
            parts = [p for p in range(2) if on(i + 1 - p)]
            return slice(parts[0], parts[-1] + 1) if parts else None

        def experts(eng, expert):
            expert(0, 0)
            expert(1, 1)
            with eng.Fori(1, E // 2) as pair:
                for s in range(2):
                    expert(pair * 2 + s, s)

        def chunk13(c):
            return (c * C13, C13 if c < FC - 1 else T13)

        def chunk2(c):
            return (W13 + c * D, D)

        def rows2(c):
            return P if c < FC - 1 else FT

        def first_chunk(i):
            return not isinstance(i, int) or 0 <= i - 2 < FC

        def first13(c):
            a, n = chunk13(c) if isinstance(c, int) else (c * C13, C13)
            return slice(a, a + n) if isinstance(c, int) else bass.ds(a, n)

        def first2(c):
            rows = slice(0, rows2(c) if isinstance(c, int) else P)
            return rows, slice(W13 + c * D, W13 + (c + 1) * D) if isinstance(c, int) else bass.ds(c * D + W13, D)

        def raw_count(e, s):
            return (e // 2 + 1) * 16 if isinstance(e, int) else (e - s) * 8 + 16

        def x2_view(x2, j):
            return x2[:, :].rearrange("p (e kt i j) -> p kt e i j", e=E, kt=2 * KT, i=POS)[:, :, :, :, bass.ds(j, 1)].rearrange(
                "p kt e i j -> p kt e (i j)")

        def seqs_of(b, t):
            return b[:, :].rearrange("p (k n) -> p k n", k=KT)[:, :, t * S:(t + 1) * S]

        def xt2_src(b=xt2_ps):
            return b[:, :].rearrange("p (kt e i) -> p kt e i", kt=2 * KT, e=E)

        @block.sync
        def _(sp):
            sp.dma_start(ids_raw[:, :], ids).then_inc(ids_in, 16)
            sp.dma_start(lr_raw, low_rank.rearrange("p (a n) -> p a n", a=2)).then_inc(lr_in, 16)
            wa_raw = raw[1][:, 0:KT * WCOLS].rearrange("p (k n) -> p k n", k=KT)
            wa_dram = w_attn.rearrange("(k p) n -> p k n", p=P)
            sp.dma_start(wa_raw[:, :, 0:WQK], wa_dram[:, :, 0:WQK]).then_inc(wa_in, 16)
            sp.dma_start(gn_sb[:, :], g_norm).then_inc(gn_in, 16)
            for t in range(2):
                sp.wait_ge(open_gathered[t], 16)
            sp.dma_start(wa_raw[:, :, WQK:WCOLS], wa_dram[:, :, WQK:WCOLS]).then_inc(wa_rest_in, 16)
            for t in range(2):
                sp.wait_ge(gathered[t], 16)
            sp.dma_start(raw[1][:, KT * WCOLS:KT * WCOLS + H * D].rearrange("p (h n) -> p h n", h=H),
                         w_o.rearrange("(h p) n -> p h n", p=P)).then_inc(wo_in, 16)

            def of_expert(w, e, cols=slice(None)):
                if isinstance(e, int):
                    return w[e, :, cols]
                return w[bass.ds(e, 1), :, cols].rearrange("e p n -> p (e n)")

            def load_expert(e, s, refill=False):
                if refill:
                    sp.wait_ge(w13_lo_done, (e - 2) * FC + FC // 2)
                sp.dma_start(raw[s][:, 0:HALF13], of_expert(w13, e, slice(0, HALF13))).then_inc(raw13a_in[s], 16)
                if refill:
                    sp.wait_ge(w13_lo_done, (e - 1) * FC)
                sp.dma_start(raw[s][:, HALF13:W13], of_expert(w13, e, slice(HALF13, W13))).then_inc(raw13b_in[s], 16)
                if refill:
                    sp.wait_ge(w2_lo_done, (e - 1) * FC)
                sp.dma_start(raw[s][:, W13:W13 + (FC - 1) * D], of_expert(w2_main, e)).then_inc(raw2_in[s], 16)
                sp.dma_start(raw[s][0:FT, W13 + (FC - 1) * D:RAW], of_expert(w2_tail, e)).then_inc(raw2_in[s], 16)

            load_expert(0, 0)
            sp.wait_ge(wa_lo_done, 3)
            load_expert(1, 1)

            def store_h2(j):
                sp.wait_ge(h2_done, j + 1)
                sp.dma_start(scratch[:, :, bass.ds(j, 1), :].rearrange("t p j d -> p t (j d)"),
                             Hres[:, bass.ds(j * 2, 2), :]).then_inc(h2_stored, 16)

            with sp.Fori(0, NP) as j:
                store_h2(j)
            sp.wait_ge(h2_stored, 16 * NP)

            def load_residual(e, s):
                sp.dma_start(h_res[:, s, :].rearrange("p (t d) -> p t d", t=2),
                             scratch[:, bass.ds(e * POS, POS), :, :].rearrange("t i j d -> (i j) t d")
                             ).then_inc(res_in[s], 16)

            def store_out(e, s):
                sp.wait_ge(y_done, e + 1)
                sp.dma_start(of_expert(out, e), y_out[:, s, :]).then_inc(stored[s], 16)

            load_expert(2, 0, refill=True)

            sp.wait_ge(x2lo_done, NP)
            load_residual(0, 0)
            load_residual(1, 1)

            def expert(e, s):
                if not isinstance(e, int) or e + 2 < E:
                    load_expert(e + 2, s, refill=True)
                store_out(e - 1, 1 - s)
                if not isinstance(e, int) or e + 1 < E:
                    load_residual(e + 1, 1 - s)

            with sp.Fori(0, E // 2 - 2) as pair:
                for s in range(2):
                    expert(pair * 2 + (1 + s), 1 - s)
            for e in range(E - 3, E + 1):
                expert(e, e % 2)
            for s in range(2):
                sp.wait_ge(stored[s], 16 * (E // 2))

        @block.gpsimd
        def _(pool):
            def select(n, tile, op, fill, base, step, channel):
                pool.wait_ge(consts, n)
                nc.gpsimd.affine_select(out=tile, in_=tile, compare_op=op, fill=fill, base=base,
                                        pattern=[[step, P]], channel_multiplier=channel).then_inc(consts, 1)

            select(5, ident[:, :], ALU.not_equal, 1.0, 0, -1, 1)
            select(6, mask[:, :], ALU.is_ge, 0.0, 0, 1, -1)
            select(7, cum_w[0:CHUNK, :], ALU.is_ge, -1.0 / GATE_NORM, 0, 1, -1)
            select(8, cum_w[CHUNK:P, :], ALU.is_ge, 0.0, -CHUNK, 1, -1)
            pool.wait_ge(consts, 9)
            pool.wait_ge(ids_done, 3)

            for t in range(2):
                nc.gpsimd.indirect_dma_start(
                    open_G[:, t, :], None, table,
                    bass.IndirectOffsetOnAxis(ap=ids_ok[:, t:t + 1], axis=0)).then_inc(open_gathered[t], 16)

            def gather(j):
                if on(j):
                    for t in range(2):
                        need(pool, gathered[t], 16 * (j - 1))
                    nc.gpsimd.tensor_copy(ids_now[:, :], ids_ok[:, bass.ds(j * 2, 2)]).then_inc(ids_sel, 1)
                    if not isinstance(j, int) or j > 1:
                        pool.wait_ge(h_done, j)
                    wait_apart(pool, ids_sel, j, pool_passed)
                    for t in range(2):
                        nc.gpsimd.indirect_dma_start(
                            G[:, t, :], None, table,
                            bass.IndirectOffsetOnAxis(ap=ids_now[:, t:t + 1], axis=0)).then_inc(gathered[t], 16)

            def split_first(c):
                cols = first13(c)
                pool.wait_ge(w13_hi_done, c + 1)
                nc.gpsimd.tensor_tensor(e_lo[:, cols], raw[0][:, cols],
                                        e_hi[:, cols].bitcast(f32), ALU.subtract).then_inc(w13_lo_done, 1)

            def step(i):
                def second_rstd():
                    j = i - 2
                    need(pool, rstd2_done, j)
                    wait_apart(pool, mv2_done, j + 1, pool_passed)
                    nc.gpsimd.tensor_scalar(veps2[:, :], mv2[:, :, 1], 1.0, EPS, ALU.mult, ALU.add).then_inc(veps2_done, 1)
                    pool.wait_ge(veps2_done, j + 1)
                    need(pool, xn2_done, j)
                    nc.gpsimd.tensor_tensor(rstd2[:, :], veps2[:, :], minus_half[:, 0:2], ALU.pow).then_inc(rstd2_done, 1)
                if on(i - 2) and not late(i - 1):
                    second_rstd()
                if on(i + 1):
                    j = i + 1
                    need(pool, rstd_done, j)
                    wait_apart(pool, mv_done, j + 1, pool_passed)
                    nc.gpsimd.tensor_scalar(veps[:, :], mv[:, :, 1], 1.0, EPS, ALU.mult, ALU.add).then_inc(veps_done, 1)
                    pool.wait_ge(veps_done, j + 1)
                    need(pool, xn_done, j)
                    nc.gpsimd.tensor_tensor(rstd[:, :], veps[:, :], minus_half[:, 0:2], ALU.pow).then_inc(rstd_done, 1)
                    if not on(i - 1):
                        gather(j + 1)
                if on(i - 1):
                    j = i - 1
                    for t in range(2):
                        need(pool, rr_done, 2 * j + t - 1)
                        wait_apart(pool, ss_done, 2 * j + t + 1, pool_passed)
                        nc.gpsimd.tensor_scalar(ms[:, t, :], ss[:, t, :], 1.0 / DV, EPS, ALU.mult, ALU.add).then_inc(ms_done, 1)
                        pool.wait_ge(ms_done, 2 * j + t + 1)
                        need(pool, og_done, 2 * j + t - 1)
                        nc.gpsimd.tensor_tensor(rr[:, t, :], ms[:, t, :], minus_half[:, 0:H], ALU.pow).then_inc(rr_done, 1)
                    if late(j):
                        second_rstd()
                    if on(i + 1):
                        gather(i + 2)
                if first_chunk(i):
                    split_first(i - 2)

            gather(1)
            wa_raw = raw[1][:, 0:KT * WCOLS].rearrange("p (k n) -> p k n", k=KT)
            pool.wait_ge(wa_hi_done, 1)
            nc.gpsimd.tensor_tensor(wa_lo[:, :, 0:WQK], wa_raw[:, :, 0:WQK], wa_hi[:, :, 0:WQK].bitcast(f32),
                                    ALU.subtract).then_inc(wa_lo_done, 1)
            for t in range(2):
                wait_apart(pool, of(t, opening["mv"], mv_done), 1, pool_passed)
                nc.gpsimd.tensor_scalar(veps[:, t:t + 1], mv[:, t, 1:2], 1.0, EPS, ALU.mult, ALU.add).then_inc(
                    of(t, opening["veps"], veps_done), 1)
                pool.wait_ge(of(t, opening["veps"], veps_done), 1)
                nc.gpsimd.tensor_tensor(rstd[:, t:t + 1], veps[:, t:t + 1], minus_half[:, 0:1], ALU.pow).then_inc(
                    of(t, opening["rstd"], rstd_done), 1)
            for i in (0, 1):
                step(i)
            with pool.Fori(2, NP - 2) as i:
                step(i)
            for i in (NP - 2, NP - 1, NP):
                step(i)
            for t in range(2):
                pool.wait_ge(xn2_done, NP - 1)
                wait_apart(pool, of(t, closing["mv2"], mv2_done), 1 if t == 0 else NP, pool_passed)
                nc.gpsimd.tensor_scalar(veps2[:, t:t + 1], mv2[:, t, 1:2], 1.0, EPS, ALU.mult, ALU.add).then_inc(
                    of(t, closing["veps2"], veps2_done), 1)
                pool.wait_ge(of(t, closing["veps2"], veps2_done), 1 if t == 0 else NP)
                nc.gpsimd.tensor_tensor(rstd2[:, t:t + 1], veps2[:, t:t + 1], minus_half[:, 0:1], ALU.pow).then_inc(
                    of(t, closing["rstd2"], rstd2_done), 1)

            def expert(e, s):
                for c in range(FC):
                    a, n = chunk13(c)
                    pool.wait_ge(w13_hi_done, (e + 1) * FC + c + 1)
                    nc.gpsimd.tensor_tensor(e_lo[:, a:a + n], raw[1 - s][:, a:a + n],
                                            e_hi[:, a:a + n].bitcast(f32), ALU.subtract).then_inc(w13_lo_done, 1)

            with pool.Fori(0, E // 2 - 1) as pair:
                for s in range(2):
                    expert(pair * 2 + s, s)
            expert(E - 2, 0)

        @block.scalar
        def _(act):
            def copy(dst, src):
                return nc.scalar.activation(dst, src, ACT.Copy)

            def table_set(n):
                act.add_instruction(mybir.InstLoadActFuncSet(
                    name=nc.get_next_instruction_name(), engine=mybir.EngineType.Activation, act_func_set_id=n))

            wa_raw = raw[1][:, 0:KT * WCOLS].rearrange("p (k n) -> p k n", k=KT)
            table_set(TABLE_LN_EXP)
            act.wait_ge(ones_done, 1)
            act.wait_ge(lr_in, 16)
            copy(lr_w[:, :, :], lr_raw).then_inc(lr_hi_done, 1)
            act.wait_ge(wa_in, 16)
            copy(wa_hi[:, :, 0:WQK], wa_raw[:, :, 0:WQK]).then_inc(wa_hi_done, 1)

            for t in range(2):
                cols = slice(t * S, (t + 1) * S)
                src = lr_in_bank(open_lr[t])
                act.wait_ge(of(t, opening["lrx"], lrx_done), 1)
                copy(lr_x[0:RANK, 0, cols], src[:, 0, cols]).then_inc(of(t, opening["lrx_hi"], lrx_hi_done), 1)
                act.wait_ge(of(t, opening["lrx_hi"], lrx_hi_done), 1)
                copy(lr_x[2 * BLK:2 * BLK + RANK, 0, cols], lr_x[0:RANK, 0, cols].bitcast(f32)).then_inc(
                    of(t, opening["lrx_dup"], lrx_dup_done), 1)
            for t in range(2):
                act.wait_ge(of(t, opening["xt"], xt_done), 1)
                copy(x_hi[:, :, t * S:(t + 1) * S], seqs_of(open_xt[t], t)).then_inc(of(t, opening["xhi"], xhi_done), 1)

            def step(i):
                en, fw, bk, cc = i + 1, i, i - 1, i - 2
                if on(fw) and not opened(fw):
                    j = fw
                    act.wait_ge(xt_done, j + 1)
                    need(act, v_done, 2 * j)
                    copy(x_hi[:, :, :].rearrange("p k n -> p (k n)"), xt_ps[:, :]).then_inc(xhi_done, 1)
                if isinstance(i, int) and i == 0:
                    act.wait_ge(wa_rest_in, 16)
                    copy(wa_hi[:, :, WQK:], wa_raw[:, :, WQK:]).then_inc(wa_hi_done, 1)
                parts = rank_parts(i)
                if parts:
                    act.wait_ge(lrx_done, i + 2)
                    need(act, lora_done, least(i + 1, NP))
                    need(act, z_done, i)
                    copy(lr_x[0:RANK, parts, :], lr_ps[:, parts, :]).then_inc(lrx_hi_done, 1)
                    act.wait_ge(lrx_hi_done, i + 2)
                    copy(lr_x[2 * BLK:2 * BLK + RANK, parts, :], lr_x[0:RANK, parts, :].bitcast(f32)).then_inc(lrx_dup_done, 1)
                if first_chunk(i):
                    c = i - 2
                    act.wait_ge(raw13a_in[0], 16)
                    act.wait_ge(raw13b_in[0], 16)
                    act.wait_ge(raw2_in[0], 32)
                    copy(e_hi[:, first13(c)], raw[0][:, first13(c)]).then_inc(w13_hi_done, 1)
                    rows, cols = first2(c)
                    copy(e_hi[rows, cols], raw[0][rows, cols]).then_inc(w2_hi_done, 1)

                def square(t):
                    j = bk
                    act.wait_ge(pv_done, 2 * j + t + 1)
                    need(act, ss_done, 2 * j + t)
                    nc.scalar.activation(sq[:, :], o_ps[t][:, :], ACT.Square).then_inc(sq_done, 1)

                def o_high(t):
                    j = bk
                    act.wait_ge(ot_done, 2 * j + t + 1)
                    need(act, wo_done, j)
                    copy(o_hi[:, t, :, :].rearrange("p h n -> p (h n)"), o_ps[t][:, :]).then_inc(ohi_done, 1)

                def v_copy(t):
                    j = fw
                    act.wait_ge(v_done, 2 * j + t + 1)
                    need(act, pv_done, 2 * j + t - 1)
                    copy(v_sb[:, t, :], v_ps[:, :]).then_inc(v_copied, 1)

                def silu(j, t):
                    act.wait_ge(g_done, 2 * j + t + 1)
                    need(act, og_done, 2 * j + t - 1)
                    nc.scalar.activation(sg[:, t, :], gate_bank(j, t)[:, :], ACT.Silu).then_inc(silu_done, 1)

                def x2_high():
                    j = cc
                    act.wait_ge(xt2_done, j + 1)
                    copy(x2_view(x2_hi, j), xt2_src()).then_inc(x2hi_done, 1)
                if on(fw) and not opened(fw):
                    table_set(TABLE_LN_EXP)
                if on(bk):
                    square(0)
                if on(cc) and not late(bk):
                    x2_high()
                if on(fw):
                    j = fw
                    act.wait_ge(z_done, j + 1)
                    need(act, gk_done, j)
                    nc.scalar.activation(lsig[:, :], z_ps[:, :], ACT.Abs).then_inc(abs_done, 1)
                    act.wait_ge(abs_done, j + 1)
                    nc.scalar.activation(lsig[:, :], lsig[:, :], ACT.Exp, scale=-1.0).then_inc(exp_done, 1)
                    act.wait_ge(exp_done, j + 1)
                    nc.scalar.activation(lsig[:, :], lsig[:, :], ACT.Ln, bias=1.0).then_inc(ln_done, 1)
                if on(bk):
                    square(1)
                    if late(bk):
                        silu(bk, 0)
                        silu(bk, 1)
                if on(fw):
                    v_copy(0)
                if on(bk):
                    o_high(0)
                if on(fw):
                    j = fw
                    act.wait_ge(cum_done, j + 1)
                    need(act, qg_done, j)
                    nc.scalar.activation(e_pos[:, :, :].rearrange("p k n -> p (k n)"), cum_ps[:, :], ACT.Exp).then_inc(epos_done, 1)
                    need(act, kg_done, j)
                    nc.scalar.activation(e_neg[:, :, :].rearrange("p k n -> p (k n)"), cum_ps[:, :], ACT.Exp, scale=-1.0).then_inc(eneg_done, 1)
                    table_set(TABLE_SILU)
                    if not late(fw):
                        silu(fw, 0)
                    v_copy(1)
                    if not late(fw):
                        silu(fw, 1)
                if on(bk):
                    o_high(1)
            for i in (0, 1):
                step(i)
            with act.Fori(2, NP - 1) as i:
                step(i)
            for i in (NP - 1, NP):
                step(i)

            act.wait_ge(xt2_done, NP - 1)
            copy(x2_view(x2_hi, NP - 2), xt2_src()).then_inc(x2hi_done, 1)
            for t in range(2):
                act.wait_ge(of(t, closing["xt2"], xt2_done), 1 if t == 0 else NP)
                copy(x2_view(x2_hi, NP - 1)[:, t::2], xt2_src(close_xt2[t])[:, t::2]).then_inc(
                    of(t, closing["x2hi"], x2hi_done), 1)

            def w13_high(e, s, c):
                a, n = chunk13(c)
                if c == 0:
                    act.wait_ge(raw13a_in[1 - s], raw_count(e + 1, 1 - s))
                if c == FC // 2:
                    act.wait_ge(raw13b_in[1 - s], raw_count(e + 1, 1 - s))
                act.wait_ge(up_done, e * FC + c + 1)
                copy(e_hi[:, a:a + n], raw[1 - s][:, a:a + n]).then_inc(w13_hi_done, 1)

            def w2_high(e, s, c):
                a, n = chunk2(c)
                if c == 0:
                    act.wait_ge(raw2_in[1 - s], raw_count(e + 1, 1 - s) * 2)
                act.wait_ge(down_done, e * FC + c + 1)
                copy(e_hi[0:rows2(c), a:a + n], raw[1 - s][0:rows2(c), a:a + n]).then_inc(w2_hi_done, 1)

            def expert(e, s, before=True, after=True):
                for c in range(FC):
                    n = e * FC + c
                    r = rows2(c)
                    act.wait_ge(up_done, n + 1)
                    need(act, mul_done, n - 2)
                    w = c % 3 * ET
                    nc.scalar.activation(s_act[0:r, w:w + ET], gu_ps[c % 3][0:r, 0:ET], ACT.Silu).then_inc(act_done, 1)
                    if after:
                        w13_high(e, s, c)
                    if c >= 2 and after:
                        w2_high(e, s, c - 2)
                    if c < 2 and before:
                        w2_high(e - 1, 1 - s, FC - 2 + c)

            expert(0, 0, before=False)
            expert(1, 1)
            with act.Fori(1, E // 2 - 1) as pair:
                for s in range(2):
                    expert(pair * 2 + s, s)
            expert(E - 2, 0)
            expert(E - 1, 1, after=False)

        @block.vector
        def _(dve):
            nc.vector.memset(ident[:, :], 0.0).then_inc(consts, 1)
            nc.vector.memset(mask[:, :], float(DK) ** -0.5).then_inc(consts, 1)
            nc.vector.memset(cum_w[0:CHUNK, :], 0.0).then_inc(consts, 1)
            nc.vector.memset(cum_w[CHUNK:P, :], 1.0 / GATE_NORM).then_inc(consts, 1)
            nc.vector.memset(minus_half[:, :], -0.5).then_inc(consts, 1)
            nc.vector.memset(lr_x[:, :, :].bitcast(f32), 1.0).then_inc(ones_done, 1)
            dve.wait_ge(ids_in, 16)
            nc.vector.tensor_scalar(ids_f[:, :], ids_raw[:, :], 0.0, float(VOCAB), ALU.is_lt, ALU.mult).then_inc(ids_done, 1)
            dve.wait_ge(ids_done, 1)
            nc.vector.tensor_tensor(ids_f[:, :], ids_raw[:, :], ids_f[:, :], ALU.add).then_inc(ids_done, 1)
            dve.wait_ge(ids_done, 2)
            nc.vector.tensor_scalar(ids_ok[:, :], ids_f[:, :], 0.0, float(VOCAB - 1), ALU.max, ALU.min).then_inc(ids_done, 1)

            wa_raw = raw[1][:, 0:KT * WCOLS].rearrange("p (k n) -> p k n", k=KT)
            wo_raw = raw[1][:, KT * WCOLS:KT * WCOLS + H * D]
            wo_hi2 = wo_hi[:, :, :].rearrange("p h n -> p (h n)")
            wo_lo2 = wo_lo[:, :, :].rearrange("p h n -> p (h n)")
            wo_scaled, wo_hi_done = sem("wo_scaled"), sem("wo_hi_done")

            def wa_low(part, cols):
                dve.wait_ge(wa_hi_done, part)
                nc.vector.tensor_tensor(wa_lo[:, :, cols], wa_raw[:, :, cols],
                                        wa_hi[:, :, cols].bitcast(f32), ALU.subtract).then_inc(wa_lo_done, 1)

            dve.wait_ge(lr_hi_done, 1)
            nc.vector.tensor_tensor(lr_w[2 * BLK:, :, :], lr_raw[2 * BLK:, :, :],
                                    lr_w[2 * BLK:, :, :].bitcast(f32), ALU.subtract).then_inc(lr_lo_done, 1)

            def norm(src, j, stats, mv, bn_done, mv_done, rstd_done, xn_done):
                for t in range(2):
                    last = nc.vector.bn_stats(stats[:, t, :], src[:, bass.ds(2 * j + t, 1), :].rearrange("p o d -> p (o d)"))
                last.then_inc(bn_done, 1)
                need(dve, rstd_done, j)
                need(dve, xn_done, j)
                wait_apart(dve, bn_done, j + 1, dve_passed)
                for t in range(2):
                    last = nc.vector.bn_aggr(mv[:, t, :], stats[:, t, :])
                last.then_inc(mv_done, 1)

            def normed(dst, src, j, mv, rstd, xn_done):
                for t in range(2):
                    last = nc.vector.tensor_scalar(
                        dst[:, t, :], src[:, bass.ds(2 * j + t, 1), :].rearrange("p o d -> p (o d)"),
                        mv[:, t, 0:1], rstd[:, t:t + 1], ALU.subtract, ALU.mult)
                last.then_inc(xn_done, 1)

            def open_lr_low(t):
                cols = slice(t * S, (t + 1) * S)
                dve.wait_ge(of(t, opening["lrx_hi"], lrx_hi_done), 1)
                nc.vector.tensor_tensor(lr_x[BLK:BLK + RANK, 0, cols], lr_in_bank(open_lr[t])[:, 0, cols],
                                        lr_x[0:RANK, 0, cols].bitcast(f32), ALU.subtract).then_inc(
                    of(t, opening["lrx_lo"], lrx_lo_done), 1)

            def open_h(t):
                dve.wait_ge(of(t, opening["lora"], lora_done), 1)
                dve.wait_ge(open_gathered[t], 16)
                nc.vector.tensor_tensor(Hres[:, t, :], open_G[:, t, 0:D], open_lora[t][:, t * D:(t + 1) * D],
                                        ALU.add).then_inc(of(t, opening["h"], h_done), 1)

            def one_bn(stats, t, row, ready, count, done):
                wait_apart(dve, ready, count, dve_passed)
                nc.vector.bn_stats(stats[:, t, :], Hres[:, row, :]).then_inc(done, 1)

            def one_aggr(mv, stats, t, ready, count, done):
                wait_apart(dve, ready, count, dve_passed)
                nc.vector.bn_aggr(mv[:, t, :], stats[:, t, :]).then_inc(done, 1)

            def one_normed(dst, t, row, mv, rstd, ready, count, done):
                dve.wait_ge(ready, count)
                nc.vector.tensor_scalar(dst[:, t, :], Hres[:, row, :], mv[:, t, 0:1], rstd[:, t:t + 1],
                                        ALU.subtract, ALU.mult).then_inc(done, 1)

            open_lr_low(0)
            open_h(0)
            open_lr_low(1)
            for t in range(2):
                one_bn(stats, t, t, of(t, opening["h"], h_done), 1, of(t, opening["bn"], bn_done))
                if t == 0:
                    open_h(1)
                one_aggr(mv, stats, t, of(t, opening["bn"], bn_done), 1, of(t, opening["mv"], mv_done))
            for t in range(2):
                one_normed(xn, t, t, mv, rstd, of(t, opening["rstd"], rstd_done), 1, of(t, opening["xn"], xn_done))
            for t in range(2):
                cols = slice(t * S, (t + 1) * S)
                dve.wait_ge(of(t, opening["xhi"], xhi_done), 1)
                last = nc.vector.tensor_tensor(x_lo[:, :, cols], seqs_of(open_xt[t], t), x_hi[:, :, cols].bitcast(f32),
                                               ALU.subtract)
            last.then_inc(xlo_done, 1)

            def step(i):
                en, fw, bk, cc = i + 1, i, i - 1, i - 2

                def mask_scores():
                    j = bk
                    dve.wait_ge(a_done, j + 1)
                    dve.wait_ge(consts, 9)
                    need(dve, pv_done, 2 * j)
                    for r in range(2):
                        nc.vector.tensor_tensor(
                            am[:, r, :, :, :].rearrange("p a b t -> p (a b) t"),
                            a_ps[r][:, :].rearrange("p (n t) -> p n t", t=P),
                            mask[:, :].unsqueeze(1).broadcast_to([P, 4, P]), ALU.mult).then_inc(am_done, 1)

                if on(fw) and not opened(fw):
                    dve.wait_ge(xhi_done, fw + 1)
                    nc.vector.tensor_tensor(x_lo[:, :, :].rearrange("p k n -> p (k n)"), xt_ps[:, :],
                                            x_hi[:, :, :].rearrange("p k n -> p (k n)").bitcast(f32),
                                            ALU.subtract).then_inc(xlo_done, 1)
                if isinstance(i, int) and i == 0:
                    wa_low(2, slice(WQK, WCOLS))
                if on(bk):
                    mask_scores()

                def second_normed():
                    j = cc
                    dve.wait_ge(rstd2_done, j + 1)
                    need(dve, xt2_done, j)
                    normed(xn2, Hres, j, mv2, rstd2, xn2_done)
                if on(cc):
                    j = cc
                    dve.wait_ge(wo_done, j + 1)
                    rows = Hres[:, bass.ds(2 * j, 2), :]
                    nc.vector.tensor_tensor(rows, rows, wo_ps[:, :].rearrange("p (t d) -> p t d", t=2), ALU.add).then_inc(h2_done, 1)
                    need(dve, mv2_done, j)
                    wait_apart(dve, h2_done, j + 1, dve_passed)
                    norm(Hres, j, stats2, mv2, bn2_done, mv2_done, rstd2_done, xn2_done)
                parts = rank_parts(i)
                if parts:
                    dve.wait_ge(lrx_hi_done, i + 2)
                    nc.vector.tensor_tensor(lr_x[BLK:BLK + RANK, parts, :], lr_ps[:, parts, :],
                                            lr_x[0:RANK, parts, :].bitcast(f32), ALU.subtract).then_inc(lrx_lo_done, 1)
                if on(cc) and not late(bk):
                    second_normed()
                if on(en):
                    j = en
                    dve.wait_ge(lora_done, j + 1)
                    for t in range(2):
                        dve.wait_ge(gathered[t], 16 * j)
                    nc.vector.tensor_tensor(Hres[:, bass.ds(2 * j, 2), :], G[:, :, 0:D],
                                            lora_ps[:, :].rearrange("p (t d) -> p t d", t=2), ALU.add).then_inc(h_done, 1)
                    need(dve, mv_done, j)
                    wait_apart(dve, h_done, j + 1, dve_passed)
                    norm(Hres, j, stats, mv, bn_done, mv_done, rstd_done, xn_done)
                def sums(t):
                    j = bk
                    dve.wait_ge(sq_done, 2 * j + t + 1)
                    need(dve, ms_done, 2 * j + t - 1)
                    nc.vector.tensor_reduce(ss[:, t, :], sq[:, :].rearrange("p (h n) -> p h n", h=H), AX.X,
                                            ALU.add).then_inc(ss_done, 1)

                def gated(t):
                    j = bk
                    dve.wait_ge(rr_done, 2 * j + t + 1)
                    dve.wait_ge(silu_done, 2 * j + t + 1)
                    need(dve, ot_done, 2 * j + t - 1)
                    for h in range(H):
                        cols = slice(h * DV, (h + 1) * DV)
                        last = nc.vector.scalar_tensor_tensor(og[:, t, cols], o_ps[t][:, cols], rr[:, t, h:h + 1],
                                                              sg[:, t, cols], ALU.mult, ALU.mult)
                    last.then_inc(og_done, 1)

                def o_low(t):
                    j = bk
                    dve.wait_ge(ohi_done, 2 * j + t + 1)
                    nc.vector.tensor_tensor(o_lo[:, t, :, :].rearrange("p h n -> p (h n)"), o_ps[t][:, :],
                                            o_hi[:, t, :, :].rearrange("p h n -> p (h n)").bitcast(f32),
                                            ALU.subtract).then_inc(olo_done, 1)

                def x2_low():
                    j = cc
                    dve.wait_ge(x2hi_done, j + 1)
                    nc.vector.tensor_tensor(x2_view(x2_lo, j), xt2_src(), x2_view(x2_hi, j).bitcast(f32),
                                            ALU.subtract).then_inc(x2lo_done, 1)
                if on(bk):
                    sums(0)
                if on(cc) and not late(bk):
                    x2_low()
                if on(fw):
                    j = fw
                    dve.wait_ge(ln_done, j + 1)
                    need(dve, cum_done, j)
                    nc.vector.scalar_tensor_tensor(gk[:, :, :].rearrange("p a b -> p (a b)"), z_ps[:, :], 0.0,
                                                   lsig[:, :], ALU.min, ALU.subtract).then_inc(gk_done, 1)
                if on(bk):
                    if late(bk):
                        sums(1)
                    gated(0)
                    if not late(bk):
                        sums(1)
                if on(en):
                    j = en
                    dve.wait_ge(rstd_done, j + 1)
                    need(dve, xt_done, j)
                    normed(xn, Hres, j, mv, rstd, xn_done)
                if on(bk):
                    if late(bk):
                        gated(1)
                        o_low(0)
                        second_normed()
                    else:
                        o_low(0)
                        gated(1)
                if on(fw):
                    j = fw
                    dve.wait_ge(epos_done, j + 1)
                    dve.wait_ge(q_done, j + 1)
                    need(dve, a_done, j)
                    nc.vector.tensor_tensor(qg[:, :, :].rearrange("p k n -> p (k n)"), q_ps[:, :],
                                            e_pos[:, :, :].rearrange("p k n -> p (k n)"), ALU.mult).then_inc(qg_done, 1)
                    dve.wait_ge(eneg_done, j + 1)
                    dve.wait_ge(k_done, j + 1)
                    nc.vector.tensor_tensor(kg[:, :, :].rearrange("p k n -> p (k n)"), k_ps[:, :],
                                            e_neg[:, :, :].rearrange("p k n -> p (k n)"), ALU.mult).then_inc(kg_done, 1)
                if on(bk):
                    o_low(1)
                if first_chunk(i):
                    c = i - 2
                    rows, cols = first2(c)
                    dve.wait_ge(w2_hi_done, c + 1)
                    nc.vector.tensor_tensor(e_lo[rows, cols], raw[0][rows, cols], e_hi[rows, cols].bitcast(f32),
                                            ALU.subtract).then_inc(w2_lo_done, 1)
                if isinstance(i, int) and i == 0:
                    dve.wait_ge(wo_in, 16)
                    dve.wait_ge(gn_in, 16)
                    nc.vector.tensor_scalar(wo_raw, wo_raw, gn_sb[:, 0:1], None, ALU.mult).then_inc(wo_scaled, 1)
                    dve.wait_ge(wo_scaled, 1)
                    nc.vector.tensor_copy(wo_hi2, wo_raw).then_inc(wo_hi_done, 1)
                    dve.wait_ge(wo_hi_done, 1)
                    nc.vector.tensor_tensor(wo_lo2, wo_raw, wo_hi2.bitcast(f32), ALU.subtract).then_inc(wa_lo_done, 1)

            for i in (0, 1):
                step(i)
            with dve.Fori(2, NP - 1) as i:
                step(i)
            for i in (NP - 1, NP):
                step(i)

            row = 2 * (NP - 1)

            def close_h2(t):
                dve.wait_ge(of(t, closing["wo"], wo_done), 1 if t == 0 else NP)
                nc.vector.tensor_tensor(Hres[:, row + t, :], Hres[:, row + t, :], close_wo[t][:, t * D:(t + 1) * D],
                                        ALU.add).then_inc(of(t, closing["h2"], h2_done), 1)

            close_h2(0)
            one_bn(stats2, 0, row, closing["h2"], 1, closing["bn2"])
            dve.wait_ge(x2hi_done, NP - 1)
            nc.vector.tensor_tensor(x2_view(x2_lo, NP - 2), xt2_src(), x2_view(x2_hi, NP - 2).bitcast(f32),
                                    ALU.subtract).then_inc(x2lo_done, 1)
            dve.wait_ge(xn2_done, NP - 1)
            one_aggr(mv2, stats2, 0, closing["bn2"], 1, closing["mv2"])
            close_h2(1)
            one_bn(stats2, 1, row + 1, h2_done, NP, bn2_done)
            one_aggr(mv2, stats2, 1, bn2_done, NP, mv2_done)
            dve.wait_ge(xt2_done, NP - 1)
            for t in range(2):
                one_normed(xn2, t, row + t, mv2, rstd2, of(t, closing["rstd2"], rstd2_done), 1 if t == 0 else NP,
                           of(t, closing["xn2"], xn2_done))
            for t in range(2):
                dve.wait_ge(of(t, closing["x2hi"], x2hi_done), 1 if t == 0 else NP)
                last = nc.vector.tensor_tensor(x2_view(x2_lo, NP - 1)[:, t::2], xt2_src(close_xt2[t])[:, t::2],
                                               x2_view(x2_hi, NP - 1)[:, t::2].bitcast(f32), ALU.subtract)
            last.then_inc(x2lo_done, 1)

            def w2_low(e, s, c):
                a, n = chunk2(c)
                r = rows2(c)
                dve.wait_ge(w2_hi_done, (e + 1) * FC + c + 1)
                nc.vector.tensor_tensor(e_lo[0:r, a:a + n], raw[1 - s][0:r, a:a + n],
                                        e_hi[0:r, a:a + n].bitcast(f32), ALU.subtract).then_inc(w2_lo_done, 1)

            def result(e, s):
                dve.wait_ge(down_done, (e + 1) * FC)
                dve.wait_ge(res_in[s], (e // 2 + 1) * 16 if isinstance(e, int) else (e - s) * 8 + 16)
                need(dve, stored[s], (e // 2) * 16 if isinstance(e, int) else (e - s) * 8)
                for t in range(2):
                    last = nc.vector.tensor_tensor(y_out[:, s, t * D:(t + 1) * D], y_ps[t][:, 0:D],
                                                   h_res[:, s, t * D:(t + 1) * D], ALU.add)
                last.then_inc(y_done, 1)

            def expert(e, s, before=True, after=True):
                for c in range(FC):
                    n = e * FC + c
                    r = rows2(c)
                    w = c % 3 * ET
                    if c == 1 and before:
                        result(e - 1, 1 - s)
                    dve.wait_ge(act_done, n + 1)
                    need(dve, hlo_done, n - 2)
                    up = gu_ps[c % 3][:, ET:2 * ET] if r == P else gu_ps[c % 3][FT:2 * FT, 0:ET]
                    nc.vector.tensor_tensor(h32[0:r, w:w + ET], s_act[0:r, w:w + ET], up, ALU.mult).then_inc(mul_done, 1)
                    dve.wait_ge(mul_done, n + 1)
                    need(dve, down_done, n - 2)
                    nc.vector.tensor_copy(h_hi[0:r, w:w + ET], h32[0:r, w:w + ET]).then_inc(hhi_done, 1)
                    dve.wait_ge(hhi_done, n + 1)
                    nc.vector.tensor_tensor(h_lo[0:r, w:w + ET], h32[0:r, w:w + ET],
                                            h_hi[0:r, w:w + ET].bitcast(f32), ALU.subtract).then_inc(hlo_done, 1)
                    if c >= 2 and after:
                        w2_low(e, s, c - 2)
                    if c < 2 and before:
                        w2_low(e - 1, 1 - s, FC - 2 + c)

            expert(0, 0, before=False)
            expert(1, 1)
            with dve.Fori(1, E // 2 - 1) as pair:
                for s in range(2):
                    expert(pair * 2 + s, s)
            expert(E - 2, 0)
            expert(E - 1, 1, after=False)
            result(E - 1, 1)

        @block.tensor
        def _(pe):
            mm = nc.tensor.matmul

            def split_mm(out, w_pairs, x_pairs):
                n = len(w_pairs)
                for k, ((wh, wl), (xh, xl)) in enumerate(zip(w_pairs, x_pairs)):
                    mm(out, wh, xh, start=k == 0, stop=False)
                    mm(out, wh, xl, start=False, stop=False)
                    last = mm(out, wl, xh, start=False, stop=k == n - 1)
                return last

            COL_Q, COL_K, COL_G, COL_V = RANK, RANK + D, RANK + 2 * D, RANK + 2 * D + NV

            def weights(c0, n):
                return [(wa_hi[:, k, c0:c0 + n], wa_lo[:, k, c0:c0 + n]) for k in range(KT)]

            def tokens(c0, n):
                return [(x_hi[:, k, c0:c0 + n], x_lo[:, k, c0:c0 + n]) for k in range(KT)]

            pe.wait_ge(consts, 9)

            def output_projection(j, t, wo_ps=wo_ps):
                if isinstance(j, int) and j == 0:
                    pe.wait_ge(wa_lo_done, 3)
                need(pe, silu_done, min(2 * j + 3, 2 * NP - 2 + 2 * late(j)) if isinstance(j, int) else 2 * j + 3)
                pe.wait_ge(olo_done, 2 * j + t + 1)
                return split_mm(wo_ps[:, t * D:(t + 1) * D],
                                [(o_hi[:, t, h, :], o_lo[:, t, h, :]) for h in range(H)],
                                [(wo_hi[:, h, :], wo_lo[:, h, :]) for h in range(H)])

            def xt2(j):
                pe.wait_ge(xn2_done, j + 1)
                pe.wait_ge(lrx_lo_done, least(j + 4, NP + 1))
                need(pe, x2lo_done, j)
                for t in range(2):
                    for k in range(KT):
                        last = nc.tensor.transpose(xt2_ps[:, k * PT + t * S:k * PT + (t + 1) * S],
                                                   xn2[:, t, k * P:(k + 1) * P], ident[:, :])
                last.then_inc(xt2_done, 1)
            for t in range(2):
                cols = slice(t * S, (t + 1) * S)
                pe.wait_ge(open_gathered[t], 16)
                nc.tensor.transpose(lr_in_bank(open_lr[t])[:, 0, cols], open_G[:, t, D:TW], ident[:, :]).then_inc(
                    of(t, opening["lrx"], lrx_done), 1)
                if t == 0:
                    pe.wait_ge(lr_lo_done, 1)
                pe.wait_ge(of(t, opening["lrx_dup"], lrx_dup_done), 1)
                pe.wait_ge(of(t, opening["lrx_lo"], lrx_lo_done), 1)
                mm(open_lora[t][:, t * D:(t + 1) * D], lr_x[0:LK, 0, cols], lr_w[0:LK, 0, :],
                   start=True, stop=True).then_inc(of(t, opening["lora"], lora_done), 1)
            for t in range(2):
                pe.wait_ge(of(t, opening["xn"], xn_done), 1)
                for k in range(KT):
                    last = nc.tensor.transpose(open_xt[t][:, k * PT + t * S:k * PT + (t + 1) * S],
                                               xn[:, t, k * P:(k + 1) * P], ident[:, :])
                last.then_inc(of(t, opening["xt"], xt_done), 1)

            def step(i):
                en, fw, bk, cc = i + 1, i, i - 1, i - 2
                if on(fw) and not opened(fw):
                    j = fw
                    pe.wait_ge(xn_done, j + 1)
                    need(pe, olo_done, 2 * j - 3)
                    for t in range(2):
                        for k in range(KT):
                            last = nc.tensor.transpose(xt_ps[:, k * PT + t * S:k * PT + (t + 1) * S],
                                                       xn[:, t, k * P:(k + 1) * P], ident[:, :])
                    last.then_inc(xt_done, 1)
                def lora():
                    j = en
                    pe.wait_ge(lrx_dup_done, i + 2)
                    pe.wait_ge(lrx_lo_done, i + 2)
                    need(pe, h2_done, j - 2)
                    for t in range(2):
                        last = mm(lora_ps[:, t * D:(t + 1) * D], lr_x[0:LK, 0, t * S:(t + 1) * S], lr_w[0:LK, 0, :],
                                  start=True, stop=True)
                    last.then_inc(lora_done, 1)

                if on(cc):
                    output_projection(cc, 0)
                if on(bk):
                    j = bk
                    pe.wait_ge(kg_done, j + 1)
                    pe.wait_ge(v_copied, 2 * j + 2)
                    for t in range(2):
                        for m in range(2):
                            for r in range(2):
                                rows = slice(r * DK, (r + 1) * DK)
                                cols = slice((t * 2 + m) * P, (t * 2 + m + 1) * P)
                                last = mm(a_ps[r][:, cols], kg[rows, m, t * S:(t + 1) * S],
                                          qg[rows, m, t * S:(t + 1) * S], start=True, stop=True)
                    last.then_inc(a_done, 1)
                if on(cc):
                    output_projection(cc, 1).then_inc(wo_done, 1)
                if on(en):
                    j = en
                    for t in range(2):
                        pe.wait_ge(gathered[t], 16 * j)
                    need(pe, silu_done, 2 * i)
                    need(pe, lrx_lo_done, i + 1)
                    for t in range(2):
                        nc.tensor.transpose(lr_ps[:, 0, t * S:(t + 1) * S], G[:, t, D:TW], ident[:, :])
                if on(fw):
                    j = fw
                    pe.wait_ge(xlo_done, j + 1)
                    if isinstance(j, int) and j == 0:
                        pe.wait_ge(wa_lo_done, 1)
                    need(pe, silu_done, 2 * j)
                    split_mm(lr_ps[:, 1, :], weights(0, RANK), tokens(0, PT)).then_inc(lrx_done, 1)
                if on(fw):
                    j = fw
                    need(pe, qg_done, j)
                    for m in range(KT):
                        last = split_mm(q_ps[:, m * PT:(m + 1) * PT], weights(COL_Q + m * P, P), tokens(0, PT))
                    last.then_inc(q_done, 1)
                if on(fw):
                    j = fw
                    need(pe, kg_done, j)
                    for m in range(KT):
                        last = split_mm(k_ps[:, m * PT:(m + 1) * PT], weights(COL_K + m * P, P), tokens(0, PT))
                    last.then_inc(k_done, 1)
                if on(en):
                    lora()

                def values(t):
                    j = bk
                    pe.wait_ge(am_done, 2 * j + 2)
                    if t == 0:
                        need(pe, xlo_done, least(j + 2, NP))
                        need(pe, olo_done, 2 * j - 1)
                    else:
                        need(pe, olo_done, 2 * j)
                    for h in range(H):
                        last = mm(o_ps[t][:, h * DV:(h + 1) * DV], am[:, h % 2, t, h // 2, :],
                                  v_sb[:, t, h * DV:(h + 1) * DV], start=True, stop=True)
                    last.then_inc(pv_done, 1)

                def output_gate(j, t):
                    if isinstance(j, int) and j == 0:
                        pe.wait_ge(wa_lo_done, 2)
                    if late(j):
                        pe.wait_ge(kg_done, NP)
                    elif t == 0:
                        need(pe, h_done, least(j + 2, NP))
                        need(pe, h2_done, j - 1)
                    else:
                        pe.wait_ge(lrx_lo_done, j + 2)
                        need(pe, x2lo_done, j - 1)
                    split_mm(gate_bank(j, t)[:, :], tokens(t * S, S), weights(COL_G, NV)).then_inc(g_done, 1)

                def v_proj(t):
                    j = fw
                    if t == 0:
                        need(pe, am_done, 2 * j)
                    else:
                        pe.wait_ge(v_copied, 2 * j + 1)
                    split_mm(v_ps[:, :], tokens(t * S, S), weights(COL_V, NV)).then_inc(v_done, 1)

                def o_transpose(t):
                    j = bk
                    pe.wait_ge(og_done, 2 * j + t + 1)
                    for h in range(H):
                        last = nc.tensor.transpose(o_ps[t][:, h * P:(h + 1) * P], og[:, t, h * DV:(h + 1) * DV], ident[:, :])
                    last.then_inc(ot_done, 1)

                if on(bk):
                    values(0)
                if on(cc) and not late(bk):
                    xt2(cc)
                if on(fw):
                    j = fw
                    pe.wait_ge(lrx_dup_done, i + 2)
                    pe.wait_ge(lrx_lo_done, i + 2)
                    need(pe, am_done, 2 * j - 1)
                    for t in range(2):
                        last = mm(z_ps[:, t * D:(t + 1) * D], lr_x[0:LK, 1, t * S:(t + 1) * S], lr_w[0:LK, 1, :],
                                  start=True, stop=True)
                    last.then_inc(z_done, 1)
                    if not on(bk):
                        v_proj(0)
                    if not late(fw):
                        output_gate(j, 0)
                if on(bk):
                    values(1)
                if late(bk):
                    output_gate(bk, 0)
                    output_gate(bk, 1)
                if on(fw) and on(bk):
                    v_proj(0)
                if on(fw):
                    j = fw
                    pe.wait_ge(gk_done, j + 1)
                    for t in range(2):
                        for m in range(KT):
                            last = mm(cum_ps[:, m * PT + t * S:m * PT + (t + 1) * S], gk[:, t, m * P:(m + 1) * P],
                                      cum_w[:, :], start=True, stop=True)
                    last.then_inc(cum_done, 1)
                if on(bk):
                    o_transpose(0)
                if on(fw):
                    v_proj(1)
                    if not late(fw):
                        output_gate(fw, 1)
                if on(bk):
                    o_transpose(1)

            steps(pe, step)

            output_projection(NP - 1, 0, close_wo[0]).then_inc(closing["wo"], 1)
            xt2(NP - 2)
            output_projection(NP - 1, 1, close_wo[1]).then_inc(wo_done, 1)
            for t in range(2):
                pe.wait_ge(of(t, closing["xn2"], xn2_done), 1 if t == 0 else NP)
                if t == 0:
                    pe.wait_ge(x2lo_done, NP - 1)
                for k in range(KT):
                    last = nc.tensor.transpose(close_xt2[t][:, k * PT + t * S:k * PT + (t + 1) * S],
                                               xn2[:, t, k * P:(k + 1) * P], ident[:, :])
                last.then_inc(of(t, closing["xt2"], xt2_done), 1)

            pe.wait_ge(x2lo_done, NP)

            def up(e, c):
                n = e * FC + c
                pe.wait_ge(w13_lo_done, n + 1)
                need(pe, mul_done, n - 2)
                a, _ = chunk13(c)
                xs = [(x2_hi[:, bass.ds(e * KT * ET + k * ET, ET)], x2_lo[:, bass.ds(e * KT * ET + k * ET, ET)])
                      for k in range(KT)]
                parts = 2 if c < FC - 1 else 1
                width = 2 * P // parts if c < FC - 1 else 2 * FT
                width = P
                for g in range(parts):
                    at = [a + k * parts * P + g * P for k in range(KT)]
                    last = split_mm(gu_ps[c % 3][:, g * ET:(g + 1) * ET],
                                    [(e_hi[:, o:o + width], e_lo[:, o:o + width]) for o in at], xs)
                last.then_inc(up_done, 1)

            def down(e, c):
                n = e * FC + c
                r = rows2(c)
                a, _ = chunk2(c)
                pe.wait_ge(hlo_done, n + 1)
                pe.wait_ge(w2_lo_done, n + 1)
                if c == 0:
                    need(pe, y_done, e)
                for t in range(2):
                    w = c % 3 * ET + t * P
                    hh, hl = h_hi[0:r, w:w + P], h_lo[0:r, w:w + P]
                    wh, wl = e_hi[0:r, a:a + D], e_lo[0:r, a:a + D]
                    mm(y_ps[t][:, 0:D], hh, wh, start=c == 0, stop=False)
                    mm(y_ps[t][:, 0:D], hh, wl, start=False, stop=False)
                    last = mm(y_ps[t][:, 0:D], hl, wh, start=False, stop=c == FC - 1)
                last.then_inc(down_done, 1)

            def expert(e, s, before=True):
                for c in range(FC):
                    up(e, c)
                    if c >= 2:
                        down(e, c - 2)
                    elif before:
                        down(e - 1, FC - 2 + c)

            expert(0, 0, before=False)
            expert(1, 1)
            with pe.Fori(1, E // 2) as pair:
                for s in range(2):
                    expert(pair * 2 + s, s)
            down(E - 1, FC - 2)
            down(E - 1, FC - 1)


def kernel(x, L0_tok_base_weight, L0_tok_lora_A, L0_tok_lora_B, L0_attn_Wq, L0_attn_Wk, L0_attn_Wv,
           L0_attn_Wg, L0_attn_gk_w1, L0_attn_gk_w2, L0_attn_gk_b2, L0_attn_g_norm_w, L0_attn_Wo,
           L0_ffn_w1, L0_ffn_w3, L0_ffn_w2):
    import numpy as np
    import concourse.bacc as bacc
    from concourse.bass_utils import run_bass_kernel_spmd

    def a(v):
        return np.asarray(v)

    def chunks(w):
        w = a(w).reshape(E, KT, P, F)
        full = w[:, :, :, :(FC - 1) * P].reshape(E, KT, P, FC - 1, P).transpose(0, 2, 3, 1, 4)
        return full, w[:, :, :, (FC - 1) * P:].transpose(0, 2, 1, 3)

    (f1, t1), (f3, t3) = chunks(L0_ffn_w1), chunks(L0_ffn_w3)
    w13 = np.concatenate([np.stack([f1, f3], 4).reshape(E, P, -1), np.stack([t1, t3], 3).reshape(E, P, -1)], 2)
    w2 = a(L0_ffn_w2)
    low_rank = np.zeros((3, BLK, 2, D), a(L0_tok_lora_B).dtype)
    low_rank[:, :RANK, 0] = a(L0_tok_lora_B)
    low_rank[:, :RANK, 1] = a(L0_attn_gk_w2)
    low_rank[0::2, RANK, 1] = a(L0_attn_gk_b2)
    low_rank = low_rank.reshape(3 * BLK, 2 * D)
    arrays = {
        "ids": a(x).T,
        "table": np.concatenate([a(L0_tok_base_weight).T, a(L0_tok_lora_A)], 1),
        "w_attn": np.concatenate([a(L0_attn_gk_w1), a(L0_attn_Wq), a(L0_attn_Wk), a(L0_attn_Wg), a(L0_attn_Wv)], 1),
        "w_o": a(L0_attn_Wo),
        "low_rank": low_rank,
        "g_norm": a(L0_attn_g_norm_w)[:, None],
        "w13": w13,
        "w2_main": w2[:, :(FC - 1) * P].reshape(E, FC - 1, P, D).transpose(0, 2, 1, 3).reshape(E, P, -1),
        "w2_tail": w2[:, (FC - 1) * P:],
    }
    arrays = {k: np.ascontiguousarray(v) for k, v in arrays.items()}
    nc = bacc.Bacc("TRN2", target_bir_lowering=False, num_devices=1)
    args = [nc.dram_tensor(k, v.shape, mybir.dt.from_np(v.dtype), kind="ExternalInput").ap() for k, v in arrays.items()]
    scratch = nc.dram_tensor("scratch", [2, S, B // 2, D], mybir.dt.float32, kind="Internal").ap()
    out = nc.dram_tensor("out", [E, P, 2 * D], mybir.dt.float32, kind="ExternalOutput").ap()
    layer_kernel(nc, *args, scratch, out)
    r = run_bass_kernel_spmd(nc, [arrays], core_ids=[0])
    y = r.results[0]["out"].reshape(E, POS, B // 2, 2, D)
    return np.ascontiguousarray(y.transpose(2, 3, 0, 1, 4)).reshape(B, S, D)
```

```python
import concourse.bass as bass
from concourse import mybir
from contextlib import ExitStack


B, S, D = 16, 128, 256
VOCAB, RANK = 8000, 16
H, DV, CHUNK = 4, 128, 64
DK = D // H
NV = H * DV
GATE_NORM, EPS = 16.0, 1e-5
E, F = 8, 704
P = 128
KT = D // P
TW = D + RANK
NP = B // 2
PT = 2 * S
FC = -(-F // P)
FT = F - (FC - 1) * P
POS = S // E
ET = B * POS
WCOLS = RANK + 2 * D + 2 * NV
WQK = RANK + 2 * D
C13 = KT * 2 * P
T13 = KT * 2 * FT
W13 = (FC - 1) * C13 + T13
HALF13 = FC // 2 * C13
RAW = W13 + FC * D
BLK = 32
LK = 2 * BLK + RANK + 1
TABLE_LN_EXP, TABLE_SILU = 6, 18


def need(eng, sem, count):
    if isinstance(count, int) and count <= 0:
        return
    eng.wait_ge(sem, count)


def wait_apart(eng, sem, count, passed):
    need(eng, sem, count)
    eng.sem_inc(passed, 1)


def least(count, top):
    return min(count, top) if isinstance(count, int) else count


def layer_kernel(nc, ids, table, w_attn, w_o, low_rank, g_norm, w13, w2,
                 scratch, out):
    f32, f32r, i32 = mybir.dt.float32, mybir.dt.float32r, mybir.dt.int32
    ALU, ACT, AX = mybir.AluOpType, mybir.ActivationFunctionType, mybir.AxisListType

    ctx = ExitStack()
    with ctx:
        def sb(name, shape, dt=f32):
            return ctx.enter_context(nc.sbuf_tensor(name, shape, dt))

        def sem(name):
            return ctx.enter_context(nc.semaphore(name))

        ident = sb("ident", [P, P])
        mask = sb("mask", [P, P])
        cum_w = sb("cum_w", [P, P])
        minus_half = sb("minus_half", [P, 8])
        lr_w = sb("lr_w", [3 * BLK, 2, D], f32r)
        gn_sb = sb("gn_sb", [P, 1])
        wa_hi = sb("wa_hi", [P, KT, WCOLS], f32r)
        wa_lo = sb("wa_lo", [P, KT, WCOLS], f32r)
        wo_hi = sb("wo_hi", [P, H, D], f32r)
        wo_lo = sb("wo_lo", [P, H, D], f32r)
        raw = [sb(f"raw{s}", [P, RAW]) for s in range(2)]
        e_hi = sb("e_hi", [P, RAW], f32r)
        e_lo = sb("e_lo", [P, RAW], f32r)
        ids_raw = sb("ids_raw", [P, B], i32)
        ids_f = sb("ids_f", [P, B])
        ids_ok = sb("ids_ok", [P, B], i32)
        ids_now = sb("ids_now", [P, 2], i32)
        G = sb("G", [P, 2, TW])
        Hres = sb("Hres", [P, B, D])
        stats = sb("stats", [P, 2, 6])
        mv = sb("mv", [P, 2, 2])
        veps = sb("veps", [P, 2])
        rstd = sb("rstd", [P, 2])
        stats2 = sb("stats2", [P, 2, 6])
        mv2 = sb("mv2", [P, 2, 2])
        veps2 = sb("veps2", [P, 2])
        rstd2 = sb("rstd2", [P, 2])
        xn = sb("xn", [P, 2, D])
        x_hi = sb("x_hi", [P, KT, PT], f32r)
        x_lo = sb("x_lo", [P, KT, PT], f32r)
        lr_x = sb("lr_x", [3 * BLK, 2, PT], f32r)
        v_sb = sb("v_sb", [P, 2, NV])
        sg = sb("sg", [P, 2, NV])
        lsig = sb("lsig", [P, 2 * D])
        gk = sb("gk", [P, 2, D])
        e_pos = sb("e_pos", [P, KT, PT])
        e_neg = sb("e_neg", [P, KT, PT])
        qg = sb("qg", [P, KT, PT])
        kg = sb("kg", [P, KT, PT])
        am = sb("am", [P, 2, 2, 2, P])
        sq = sb("sq", [P, NV])
        ss = sb("ss", [P, 2, H])
        ms = sb("ms", [P, 2, H])
        rr = sb("rr", [P, 2, H])
        og = sb("og", [P, 2, NV])
        o_hi = sb("o_hi", [P, 2, H, P], f32r)
        o_lo = sb("o_lo", [P, 2, H, P], f32r)
        xn2 = sb("xn2", [P, 2, D])
        x2_hi = sb("x2_hi", [P, E * KT * ET], f32r)
        x2_lo = sb("x2_lo", [P, E * KT * ET], f32r)

        s_act = am[:, :, :, :, :].rearrange("p a b c t -> p (a b c t)")
        h32 = og[:, :, :].rearrange("p a n -> p (a n)")
        h_hi = o_hi[:, :, :, :].rearrange("p a h t -> p (a h t)")
        h_lo = o_lo[:, :, :, :].rearrange("p a h t -> p (a h t)")
        lr_raw = sq[0:3 * BLK, :].rearrange("p (a n) -> p a n", a=2)
        open_G = og[:, :, 0:TW]
        y_out, h_res = v_sb, sg

        def lr_in_bank(b):
            return b[0:RANK, :].rearrange("p (a n) -> p a n", a=2)

        bank = [ctx.enter_context(nc.psum_tensor(f"bank{n}", [P, 512], f32)) for n in range(8)]
        q_ps, k_ps = bank[0], bank[1]
        xt_ps, xt2_ps = bank[3], bank[6]
        o_ps = [bank[3], bank[2]]
        a_ps = [bank[4], bank[5]]
        z_ps = cum_ps = bank[4]
        v_ps = bank[5]
        lr_ps = lr_in_bank(bank[6])
        lora_ps = wo_ps = bank[7]
        g_ps = [bank[7], bank[6]]
        gu_ps = [bank[0], bank[1], bank[2]]
        y_ps = [bank[3], bank[4]]

        ids_in, ids_done, consts, lr_in, wa_in, wa_rest_in, wo_in, gn_in = map(
            sem, ["ids_in", "ids_done", "consts", "lr_in", "wa_in", "wa_rest_in", "wo_in", "gn_in"])
        ids_sel = sem("ids_sel")
        gathered = [sem(f"gathered{t}") for t in range(2)]
        open_gathered = [sem(f"open_gathered{t}") for t in range(2)]
        wa_hi_done, wa_lo_done, ones_done = sem("wa_hi_done"), sem("wa_lo_done"), sem("ones_done")
        lr_hi_done, lr_lo_done = sem("lr_hi_done"), sem("lr_lo_done")
        lrx_done, lrx_hi_done, lrx_dup_done, lrx_lo_done = (
            sem("lrx_done"), sem("lrx_hi_done"), sem("lrx_dup_done"), sem("lrx_lo_done"))
        lora_done, h_done = sem("lora_done"), sem("h_done")
        bn_done, mv_done, veps_done, rstd_done, xn_done = (
            sem("bn_done"), sem("mv_done"), sem("veps_done"), sem("rstd_done"), sem("xn_done"))
        xt_done, xhi_done, xlo_done = sem("xt_done"), sem("xhi_done"), sem("xlo_done")
        z_done = sem("z_done")
        abs_done, exp_done, ln_done, gk_done = sem("abs_done"), sem("exp_done"), sem("ln_done"), sem("gk_done")
        cum_done, epos_done, eneg_done = sem("cum_done"), sem("epos_done"), sem("eneg_done")
        q_done, k_done, qg_done, kg_done = sem("q_done"), sem("k_done"), sem("qg_done"), sem("kg_done")
        v_done, v_copied, g_done, silu_done = sem("v_done"), sem("v_copied"), sem("g_done"), sem("silu_done")
        a_done, am_done, pv_done = sem("a_done"), sem("am_done"), sem("pv_done")
        sq_done, ss_done, ms_done, rr_done = sem("sq_done"), sem("ss_done"), sem("ms_done"), sem("rr_done")
        og_done, ot_done, ohi_done, olo_done = sem("og_done"), sem("ot_done"), sem("ohi_done"), sem("olo_done")
        wo_done, h2_done, h2_stored = sem("wo_done"), sem("h2_done"), sem("h2_stored")
        bn2_done, mv2_done, veps2_done, rstd2_done, xn2_done = (
            sem("bn2_done"), sem("mv2_done"), sem("veps2_done"), sem("rstd2_done"), sem("xn2_done"))
        xt2_done, x2hi_done, x2lo_done = sem("xt2_done"), sem("x2hi_done"), sem("x2lo_done")
        raw13a_in, raw13b_in, raw2_in = (
            [sem(f"{part}_in{s}") for s in range(2)] for part in ("raw13a", "raw13b", "raw2"))
        w13_hi_done, w13_lo_done = sem("w13_hi_done"), sem("w13_lo_done")
        w2_hi_done, w2_lo_done = sem("w2_hi_done"), sem("w2_lo_done")
        up_done, act_done, mul_done, hhi_done, hlo_done, down_done = (
            sem("up_done"), sem("act_done"), sem("mul_done"), sem("hhi_done"), sem("hlo_done"), sem("down_done"))
        res_in = [sem(f"res_in{s}") for s in range(2)]
        y_done = sem("y_done")
        stored = [sem(f"stored{s}") for s in range(2)]

        opening = {name: sem(f"opening_{name}") for name in
                   ("lrx", "lrx_hi", "lrx_dup", "lrx_lo", "lora", "h", "bn", "mv", "veps", "rstd", "xn", "xt", "xhi")}
        closing = {name: sem(f"closing_{name}") for name in
                   ("wo", "h2", "bn", "mv", "veps", "rstd", "xn", "xt2", "x2hi")}

        dve_passed, pool_passed = sem("dve_passed"), sem("pool_passed")

        block = ctx.enter_context(nc.Block())

        open_lr, open_lora, open_xt = [bank[6], bank[4]], [bank[7], bank[5]], [bank[3], bank[2]]
        close_wo, close_xt2 = [bank[4], bank[5]], [bank[3], bank[2]]

        def steps(eng, step):
            for i in range(3):
                step(i)
            with eng.Fori(3, NP - 1) as i:
                step(i)
            step(NP - 1)

        def on(j):
            return not isinstance(j, int) or 0 <= j < NP

        def opened(j):
            return isinstance(j, int) and j == 0

        def late(j):
            return isinstance(j, int) and j == NP - 1

        def gate_bank(j, t):
            return bank[t] if late(j) else g_ps[t]

        def of(t, first, pair):
            return pair if t else first

        def rank_parts(i):
            parts = [p for p in range(2) if on(i + 1 - p)]
            return slice(parts[0], parts[-1] + 1) if parts else None

        def chunk13(c):
            return (c * C13, C13 if c < FC - 1 else T13)

        def chunk2(c):
            return (W13 + c * D, D)

        def rows2(c):
            return P if c < FC - 1 else FT

        def first_chunk(i):
            return not isinstance(i, int) or 0 <= i - 2 < FC

        def first13(c):
            a, n = chunk13(c) if isinstance(c, int) else (c * C13, C13)
            return slice(a, a + n) if isinstance(c, int) else bass.ds(a, n)

        def first2(c):
            return slice(W13 + c * D, W13 + (c + 1) * D) if isinstance(c, int) else bass.ds(c * D + W13, D)

        def slot_count(e, s):
            return (e // 2 + 1) * 16 if isinstance(e, int) else (e - s) * 8 + 16

        def x2_view(x2, j):
            return x2[:, :].rearrange("p (e kt i j) -> p kt e i j", e=E, kt=2 * KT, i=POS)[:, :, :, :, bass.ds(j, 1)].rearrange(
                "p kt e i j -> p kt e (i j)")

        def seqs_of(b, t):
            return b[:, :].rearrange("p (k n) -> p k n", k=KT)[:, :, t * S:(t + 1) * S]

        def xt2_src(b=xt2_ps):
            return b[:, :].rearrange("p (kt e i) -> p kt e i", kt=2 * KT, e=E)

        @block.sync
        def _(sp):
            sp.dma_start(ids_raw[:, :], ids).then_inc(ids_in, 16)
            sp.dma_start(lr_raw, low_rank.rearrange("p (a n) -> p a n", a=2)).then_inc(lr_in, 16)
            for s in range(2):
                sp.sem_inc(stored[s], 16)
            wa_raw = raw[1][:, 0:KT * WCOLS].rearrange("p (k n) -> p k n", k=KT)
            wa_dram = w_attn.rearrange("(k p) n -> p k n", p=P)
            sp.dma_start(wa_raw[:, :, 0:WQK], wa_dram[:, :, 0:WQK]).then_inc(wa_in, 16)
            sp.dma_start(gn_sb[:, :], g_norm).then_inc(gn_in, 16)
            for t in range(2):
                sp.wait_ge(open_gathered[t], 16)
            sp.dma_start(wa_raw[:, :, WQK:WCOLS], wa_dram[:, :, WQK:WCOLS]).then_inc(wa_rest_in, 16)
            for t in range(2):
                sp.wait_ge(gathered[t], 16)
            sp.dma_start(raw[1][:, KT * WCOLS:KT * WCOLS + H * D].rearrange("p (h n) -> p h n", h=H),
                         w_o.rearrange("(h p) n -> p h n", p=P)).then_inc(wo_in, 16)

            def of_expert(w, e, cols=slice(None)):
                if isinstance(e, int):
                    return w[e, :, cols]
                return w[bass.ds(e, 1), :, cols].rearrange("e p n -> p (e n)")

            def load_expert(e, s, refill=False):
                if refill:
                    sp.wait_ge(w13_lo_done, (e - 2) * FC + FC // 2)
                sp.dma_start(raw[s][:, 0:HALF13], of_expert(w13, e, slice(0, HALF13))).then_inc(raw13a_in[s], 16)
                if refill:
                    sp.wait_ge(w13_lo_done, (e - 1) * FC)
                sp.dma_start(raw[s][:, HALF13:W13], of_expert(w13, e, slice(HALF13, W13))).then_inc(raw13b_in[s], 16)
                if refill:
                    sp.wait_ge(w2_lo_done, (e - 1) * FC)
                sp.dma_start(raw[s][:, W13:RAW], of_expert(w2, e)).then_inc(raw2_in[s], 16)

            load_expert(0, 0)
            sp.wait_ge(wa_lo_done, 3)
            load_expert(1, 1)

            def store_h2(j):
                sp.wait_ge(h2_done, j + 1)
                sp.dma_start(scratch[:, :, bass.ds(j, 1), :].rearrange("t p j d -> p t (j d)"),
                             Hres[:, bass.ds(j * 2, 2), :]).then_inc(h2_stored, 16)

            with sp.Fori(0, NP) as j:
                store_h2(j)
            sp.wait_ge(h2_stored, 16 * NP)

            def load_residual(e, s):
                sp.dma_start(h_res[:, s, :].rearrange("p (t d) -> p t d", t=2),
                             scratch[:, bass.ds(e * POS, POS), :, :].rearrange("t i j d -> (i j) t d")
                             ).then_inc(res_in[s], 16)

            def store_out(e, s):
                sp.wait_ge(y_done, e + 1)
                sp.dma_start(of_expert(out, e), y_out[:, s, :]).then_inc(stored[s], 16)

            load_expert(2, 0, refill=True)

            sp.wait_ge(x2lo_done, NP)
            load_residual(0, 0)
            load_residual(1, 1)

            def expert(e, s):
                if not isinstance(e, int) or e + 2 < E:
                    load_expert(e + 2, s, refill=True)
                store_out(e - 1, 1 - s)
                if not isinstance(e, int) or e + 1 < E:
                    load_residual(e + 1, 1 - s)

            with sp.Fori(0, E // 2 - 2) as pair:
                for s in range(2):
                    expert(pair * 2 + (1 + s), 1 - s)
            for e in range(E - 3, E + 1):
                expert(e, e % 2)
            for s in range(2):
                sp.wait_ge(stored[s], 16 * (E // 2 + 1))

        @block.gpsimd
        def _(pool):
            def select(n, tile, op, fill, base, step, channel):
                pool.wait_ge(consts, n)
                nc.gpsimd.affine_select(out=tile, in_=tile, compare_op=op, fill=fill, base=base,
                                        pattern=[[step, P]], channel_multiplier=channel).then_inc(consts, 1)

            select(5, ident[:, :], ALU.not_equal, 1.0, 0, -1, 1)
            select(6, mask[:, :], ALU.is_ge, 0.0, 0, 1, -1)
            select(7, cum_w[0:CHUNK, :], ALU.is_ge, -1.0 / GATE_NORM, 0, 1, -1)
            select(8, cum_w[CHUNK:P, :], ALU.is_ge, 0.0, -CHUNK, 1, -1)
            pool.wait_ge(consts, 9)
            pool.wait_ge(ids_done, 3)

            for t in range(2):
                nc.gpsimd.indirect_dma_start(
                    open_G[:, t, :], None, table,
                    bass.IndirectOffsetOnAxis(ap=ids_ok[:, t:t + 1], axis=0)).then_inc(open_gathered[t], 16)

            def gather(j):
                if on(j):
                    for t in range(2):
                        need(pool, gathered[t], 16 * (j - 1))
                    nc.gpsimd.tensor_copy(ids_now[:, :], ids_ok[:, bass.ds(j * 2, 2)]).then_inc(ids_sel, 1)
                    if not isinstance(j, int) or j > 1:
                        pool.wait_ge(h_done, j)
                    wait_apart(pool, ids_sel, j, pool_passed)
                    for t in range(2):
                        nc.gpsimd.indirect_dma_start(
                            G[:, t, :], None, table,
                            bass.IndirectOffsetOnAxis(ap=ids_now[:, t:t + 1], axis=0)).then_inc(gathered[t], 16)

            def split_first(c):
                cols = first13(c)
                pool.wait_ge(w13_hi_done, c + 1)
                nc.gpsimd.tensor_tensor(e_lo[:, cols], raw[0][:, cols],
                                        e_hi[:, cols].bitcast(f32), ALU.subtract).then_inc(w13_lo_done, 1)

            def second_rstd(j):
                need(pool, rstd2_done, j)
                wait_apart(pool, mv2_done, j + 1, pool_passed)
                nc.gpsimd.tensor_scalar(veps2[:, :], mv2[:, :, 1], 1.0, EPS, ALU.mult, ALU.add).then_inc(veps2_done, 1)
                pool.wait_ge(veps2_done, j + 1)
                need(pool, xn2_done, j)
                nc.gpsimd.tensor_tensor(rstd2[:, :], veps2[:, :], minus_half[:, 0:2], ALU.pow).then_inc(rstd2_done, 1)

            def head_scales(j, t):
                need(pool, rr_done, 2 * j + t - 1)
                wait_apart(pool, ss_done, 2 * j + t + 1, pool_passed)
                nc.gpsimd.tensor_scalar(ms[:, t, :], ss[:, t, :], 1.0 / DV, EPS, ALU.mult, ALU.add).then_inc(ms_done, 1)
                pool.wait_ge(ms_done, 2 * j + t + 1)
                need(pool, og_done, 2 * j + t - 1)
                nc.gpsimd.tensor_tensor(rr[:, t, :], ms[:, t, :], minus_half[:, 0:H], ALU.pow).then_inc(rr_done, 1)

            def step(i):
                if on(i - 2):
                    second_rstd(i - 2)
                if on(i + 1):
                    j = i + 1
                    need(pool, rstd_done, j)
                    wait_apart(pool, mv_done, j + 1, pool_passed)
                    nc.gpsimd.tensor_scalar(veps[:, :], mv[:, :, 1], 1.0, EPS, ALU.mult, ALU.add).then_inc(veps_done, 1)
                    pool.wait_ge(veps_done, j + 1)
                    need(pool, xn_done, j)
                    nc.gpsimd.tensor_tensor(rstd[:, :], veps[:, :], minus_half[:, 0:2], ALU.pow).then_inc(rstd_done, 1)
                    if not on(i - 1):
                        gather(j + 1)
                if on(i - 1):
                    j = i - 1
                    for t in range(2):
                        head_scales(j, t)
                    if on(i + 1):
                        gather(i + 2)
                if first_chunk(i):
                    split_first(i - 2)

            gather(1)
            wa_raw = raw[1][:, 0:KT * WCOLS].rearrange("p (k n) -> p k n", k=KT)
            pool.wait_ge(wa_hi_done, 1)
            nc.gpsimd.tensor_tensor(wa_lo[:, :, 0:WQK], wa_raw[:, :, 0:WQK], wa_hi[:, :, 0:WQK].bitcast(f32),
                                    ALU.subtract).then_inc(wa_lo_done, 1)
            for t in range(2):
                wait_apart(pool, of(t, opening["mv"], mv_done), 1, pool_passed)
                nc.gpsimd.tensor_scalar(veps[:, t:t + 1], mv[:, t, 1:2], 1.0, EPS, ALU.mult, ALU.add).then_inc(
                    of(t, opening["veps"], veps_done), 1)
                pool.wait_ge(of(t, opening["veps"], veps_done), 1)
                nc.gpsimd.tensor_tensor(rstd[:, t:t + 1], veps[:, t:t + 1], minus_half[:, 0:1], ALU.pow).then_inc(
                    of(t, opening["rstd"], rstd_done), 1)
            for i in range(3):
                step(i)
            with pool.Fori(3, NP - 2) as i:
                step(i)
            for i in (NP - 2, NP - 1):
                step(i)
            for t in range(2):
                head_scales(NP - 1, t)
            second_rstd(NP - 2)
            for t in range(2):
                wait_apart(pool, closing["mv"], t + 1, pool_passed)
                nc.gpsimd.tensor_scalar(veps[:, t:t + 1], mv[:, t, 1:2], 1.0, EPS, ALU.mult, ALU.add).then_inc(closing["veps"], 1)
                pool.wait_ge(closing["veps"], t + 1)
                nc.gpsimd.tensor_tensor(rstd[:, t:t + 1], veps[:, t:t + 1], minus_half[:, 0:1], ALU.pow).then_inc(closing["rstd"], 1)

            def expert(e, s):
                for c in range(FC):
                    a, n = chunk13(c)
                    pool.wait_ge(w13_hi_done, (e + 1) * FC + c + 1)
                    nc.gpsimd.tensor_tensor(e_lo[:, a:a + n], raw[1 - s][:, a:a + n],
                                            e_hi[:, a:a + n].bitcast(f32), ALU.subtract).then_inc(w13_lo_done, 1)

            with pool.Fori(0, E // 2 - 1) as pair:
                for s in range(2):
                    expert(pair * 2 + s, s)
            expert(E - 2, 0)

        @block.scalar
        def _(act):
            def copy(dst, src):
                return nc.scalar.activation(dst, src, ACT.Copy)

            def table_set(n):
                act.add_instruction(mybir.InstLoadActFuncSet(
                    name=nc.get_next_instruction_name(), engine=mybir.EngineType.Activation, act_func_set_id=n))

            wa_raw = raw[1][:, 0:KT * WCOLS].rearrange("p (k n) -> p k n", k=KT)
            table_set(TABLE_LN_EXP)
            act.wait_ge(ones_done, 1)
            act.wait_ge(lr_in, 16)
            copy(lr_w[:, :, :], lr_raw).then_inc(lr_hi_done, 1)
            act.wait_ge(wa_in, 16)
            copy(wa_hi[:, :, 0:WQK], wa_raw[:, :, 0:WQK]).then_inc(wa_hi_done, 1)

            def square(j, t):
                act.wait_ge(pv_done, 2 * j + t + 1)
                need(act, ss_done, 2 * j + t)
                nc.scalar.activation(sq[:, :], o_ps[t][:, :], ACT.Square).then_inc(sq_done, 1)

            def o_high(j, t):
                act.wait_ge(ot_done, 2 * j + t + 1)
                need(act, wo_done, j)
                copy(o_hi[:, t, :, :].rearrange("p h n -> p (h n)"), o_ps[t][:, :]).then_inc(ohi_done, 1)

            def v_copy(j, t):
                act.wait_ge(v_done, 2 * j + t + 1)
                need(act, pv_done, 2 * j + t - 1)
                copy(v_sb[:, t, :], v_ps[:, :]).then_inc(v_copied, 1)

            def silu(j, t):
                act.wait_ge(g_done, 2 * j + t + 1)
                need(act, og_done, 2 * j + t - 1)
                nc.scalar.activation(sg[:, t, :], gate_bank(j, t)[:, :], ACT.Silu).then_inc(silu_done, 1)

            def x2_high(j):
                act.wait_ge(xt2_done, j + 1)
                copy(x2_view(x2_hi, j), xt2_src()).then_inc(x2hi_done, 1)

            def log_sigmoid(j):
                act.wait_ge(z_done, j + 1)
                need(act, gk_done, j)
                nc.scalar.activation(lsig[:, :], z_ps[:, :], ACT.Abs).then_inc(abs_done, 1)
                act.wait_ge(abs_done, j + 1)
                nc.scalar.activation(lsig[:, :], lsig[:, :], ACT.Exp, scale=-1.0).then_inc(exp_done, 1)
                act.wait_ge(exp_done, j + 1)
                nc.scalar.activation(lsig[:, :], lsig[:, :], ACT.Ln, bias=1.0).then_inc(ln_done, 1)

            for t in range(2):
                cols = slice(t * S, (t + 1) * S)
                src = lr_in_bank(open_lr[t])
                act.wait_ge(of(t, opening["lrx"], lrx_done), 1)
                copy(lr_x[0:RANK, 0, cols], src[:, 0, cols]).then_inc(of(t, opening["lrx_hi"], lrx_hi_done), 1)
                act.wait_ge(of(t, opening["lrx_hi"], lrx_hi_done), 1)
                copy(lr_x[2 * BLK:2 * BLK + RANK, 0, cols], lr_x[0:RANK, 0, cols].bitcast(f32)).then_inc(
                    of(t, opening["lrx_dup"], lrx_dup_done), 1)
            for t in range(2):
                act.wait_ge(of(t, opening["xt"], xt_done), 1)
                copy(x_hi[:, :, t * S:(t + 1) * S], seqs_of(open_xt[t], t)).then_inc(of(t, opening["xhi"], xhi_done), 1)

            def step(i):
                en, fw, bk, cc = i + 1, i, i - 1, i - 2
                if on(fw) and not opened(fw):
                    j = fw
                    act.wait_ge(xt_done, j + 1)
                    need(act, v_done, 2 * j)
                    copy(x_hi[:, :, :].rearrange("p k n -> p (k n)"), xt_ps[:, :]).then_inc(xhi_done, 1)
                if isinstance(i, int) and i == 0:
                    act.wait_ge(wa_rest_in, 16)
                    copy(wa_hi[:, :, WQK:], wa_raw[:, :, WQK:]).then_inc(wa_hi_done, 1)
                parts = rank_parts(i)
                if parts:
                    act.wait_ge(lrx_done, i + 2)
                    need(act, lora_done, least(i + 1, NP))
                    need(act, z_done, i)
                    copy(lr_x[0:RANK, parts, :], lr_ps[:, parts, :]).then_inc(lrx_hi_done, 1)
                    act.wait_ge(lrx_hi_done, i + 2)
                    copy(lr_x[2 * BLK:2 * BLK + RANK, parts, :], lr_x[0:RANK, parts, :].bitcast(f32)).then_inc(lrx_dup_done, 1)
                if first_chunk(i):
                    c = i - 2
                    act.wait_ge(raw13a_in[0], 16)
                    act.wait_ge(raw13b_in[0], 16)
                    act.wait_ge(raw2_in[0], 16)
                    copy(e_hi[:, first13(c)], raw[0][:, first13(c)]).then_inc(w13_hi_done, 1)
                    cols = first2(c)
                    copy(e_hi[:, cols], raw[0][:, cols]).then_inc(w2_hi_done, 1)

                if on(fw) and not opened(fw):
                    table_set(TABLE_LN_EXP)
                if late(fw):
                    log_sigmoid(fw)
                if on(bk):
                    square(bk, 0)
                if on(cc):
                    x2_high(cc)
                if on(fw) and not late(fw):
                    log_sigmoid(fw)
                if on(bk):
                    square(bk, 1)
                if on(fw):
                    v_copy(fw, 0)
                if on(bk) and not late(fw):
                    o_high(bk, 0)
                if on(fw):
                    j = fw
                    act.wait_ge(cum_done, j + 1)
                    need(act, qg_done, j)
                    nc.scalar.activation(e_pos[:, :, :].rearrange("p k n -> p (k n)"), cum_ps[:, :], ACT.Exp).then_inc(epos_done, 1)
                    need(act, kg_done, j)
                    nc.scalar.activation(e_neg[:, :, :].rearrange("p k n -> p (k n)"), cum_ps[:, :], ACT.Exp, scale=-1.0).then_inc(eneg_done, 1)
                if late(fw):
                    v_copy(fw, 1)
                    o_high(bk, 0)
                    table_set(TABLE_SILU)
                else:
                    table_set(TABLE_SILU)
                    silu(fw, 0)
                    v_copy(fw, 1)
                    silu(fw, 1)
                    if on(bk):
                        o_high(bk, 1)

            steps(act, step)

            L, M = NP - 1, NP - 2
            o_high(M, 1)
            square(L, 0)
            square(L, 1)
            silu(L, 0)
            silu(L, 1)
            o_high(L, 0)
            o_high(L, 1)
            x2_high(M)
            for t in range(2):
                act.wait_ge(closing["xt2"], t + 1)
                copy(x2_view(x2_hi, L)[:, t::2], xt2_src(close_xt2[t])[:, t::2]).then_inc(closing["x2hi"], 1)

            def w13_high(e, s, c):
                a, n = chunk13(c)
                if c == 0:
                    act.wait_ge(raw13a_in[1 - s], slot_count(e + 1, 1 - s))
                if c == FC // 2:
                    act.wait_ge(raw13b_in[1 - s], slot_count(e + 1, 1 - s))
                act.wait_ge(up_done, e * FC + c + 1)
                copy(e_hi[:, a:a + n], raw[1 - s][:, a:a + n]).then_inc(w13_hi_done, 1)

            def w2_high(e, s, c):
                a, n = chunk2(c)
                if c == 0:
                    act.wait_ge(raw2_in[1 - s], slot_count(e + 1, 1 - s))
                act.wait_ge(down_done, e * FC + c + 1)
                copy(e_hi[:, a:a + n], raw[1 - s][:, a:a + n]).then_inc(w2_hi_done, 1)

            def expert(e, s, before=True, after=True):
                for c in range(FC):
                    n = e * FC + c
                    r = rows2(c)
                    act.wait_ge(up_done, n + 1)
                    need(act, mul_done, n - 2)
                    w = c % 3 * ET
                    nc.scalar.activation(s_act[0:r, w:w + ET], gu_ps[c % 3][0:r, 0:ET], ACT.Silu).then_inc(act_done, 1)
                    if after:
                        w13_high(e, s, c)
                    if c >= 2 and after:
                        w2_high(e, s, c - 2)
                    if c < 2 and before:
                        w2_high(e - 1, 1 - s, FC - 2 + c)

            expert(0, 0, before=False)
            expert(1, 1)
            with act.Fori(1, E // 2 - 1) as pair:
                for s in range(2):
                    expert(pair * 2 + s, s)
            expert(E - 2, 0)
            expert(E - 1, 1, after=False)

        @block.vector
        def _(dve):
            nc.vector.memset(ident[:, :], 0.0).then_inc(consts, 1)
            nc.vector.memset(mask[:, :], float(DK) ** -0.5).then_inc(consts, 1)
            nc.vector.memset(cum_w[0:CHUNK, :], 0.0).then_inc(consts, 1)
            nc.vector.memset(cum_w[CHUNK:P, :], 1.0 / GATE_NORM).then_inc(consts, 1)
            nc.vector.memset(minus_half[:, :], -0.5).then_inc(consts, 1)
            nc.vector.memset(lr_x[:, :, :].bitcast(f32), 1.0).then_inc(ones_done, 1)
            dve.wait_ge(ids_in, 16)
            nc.vector.tensor_scalar(ids_f[:, :], ids_raw[:, :], 0.0, float(VOCAB), ALU.is_lt, ALU.mult).then_inc(ids_done, 1)
            dve.wait_ge(ids_done, 1)
            nc.vector.tensor_tensor(ids_f[:, :], ids_raw[:, :], ids_f[:, :], ALU.add).then_inc(ids_done, 1)
            dve.wait_ge(ids_done, 2)
            nc.vector.tensor_scalar(ids_ok[:, :], ids_f[:, :], 0.0, float(VOCAB - 1), ALU.max, ALU.min).then_inc(ids_done, 1)

            wa_raw = raw[1][:, 0:KT * WCOLS].rearrange("p (k n) -> p k n", k=KT)
            wo_raw = raw[1][:, KT * WCOLS:KT * WCOLS + H * D]
            wo_hi2 = wo_hi[:, :, :].rearrange("p h n -> p (h n)")
            wo_lo2 = wo_lo[:, :, :].rearrange("p h n -> p (h n)")
            wo_scaled, wo_hi_done = sem("wo_scaled"), sem("wo_hi_done")

            def wa_low(part, cols):
                dve.wait_ge(wa_hi_done, part)
                nc.vector.tensor_tensor(wa_lo[:, :, cols], wa_raw[:, :, cols],
                                        wa_hi[:, :, cols].bitcast(f32), ALU.subtract).then_inc(wa_lo_done, 1)

            dve.wait_ge(lr_hi_done, 1)
            nc.vector.tensor_tensor(lr_w[2 * BLK:, :, :], lr_raw[2 * BLK:, :, :],
                                    lr_w[2 * BLK:, :, :].bitcast(f32), ALU.subtract).then_inc(lr_lo_done, 1)

            def norm(src, j, stats, mv, bn_done, mv_done, rstd_done, xn_done):
                for t in range(2):
                    last = nc.vector.bn_stats(stats[:, t, :], src[:, bass.ds(2 * j + t, 1), :].rearrange("p o d -> p (o d)"))
                last.then_inc(bn_done, 1)
                need(dve, rstd_done, j)
                need(dve, xn_done, j)
                wait_apart(dve, bn_done, j + 1, dve_passed)
                for t in range(2):
                    last = nc.vector.bn_aggr(mv[:, t, :], stats[:, t, :])
                last.then_inc(mv_done, 1)

            def normed(dst, src, j, mv, rstd, xn_done):
                for t in range(2):
                    last = nc.vector.tensor_scalar(
                        dst[:, t, :], src[:, bass.ds(2 * j + t, 1), :].rearrange("p o d -> p (o d)"),
                        mv[:, t, 0:1], rstd[:, t:t + 1], ALU.subtract, ALU.mult)
                last.then_inc(xn_done, 1)

            def mask_scores(j):
                dve.wait_ge(a_done, j + 1)
                dve.wait_ge(consts, 9)
                need(dve, pv_done, 2 * j)
                for r in range(2):
                    nc.vector.tensor_tensor(
                        am[:, r, :, :, :].rearrange("p a b t -> p (a b) t"),
                        a_ps[r][:, :].rearrange("p (n t) -> p n t", t=P),
                        mask[:, :].unsqueeze(1).broadcast_to([P, 4, P]), ALU.mult).then_inc(am_done, 1)

            def second_normed(j):
                dve.wait_ge(rstd2_done, j + 1)
                need(dve, xt2_done, j)
                normed(xn2, Hres, j, mv2, rstd2, xn2_done)

            def sums(j, t):
                dve.wait_ge(sq_done, 2 * j + t + 1)
                need(dve, ms_done, 2 * j + t - 1)
                nc.vector.tensor_reduce(ss[:, t, :], sq[:, :].rearrange("p (h n) -> p h n", h=H), AX.X,
                                        ALU.add).then_inc(ss_done, 1)

            def gated(j, t):
                dve.wait_ge(rr_done, 2 * j + t + 1)
                dve.wait_ge(silu_done, 2 * j + t + 1)
                need(dve, ot_done, 2 * j + t - 1)
                for h in range(H):
                    cols = slice(h * DV, (h + 1) * DV)
                    last = nc.vector.scalar_tensor_tensor(og[:, t, cols], o_ps[t][:, cols], rr[:, t, h:h + 1],
                                                          sg[:, t, cols], ALU.mult, ALU.mult)
                last.then_inc(og_done, 1)

            def o_low(j, t):
                dve.wait_ge(ohi_done, 2 * j + t + 1)
                nc.vector.tensor_tensor(o_lo[:, t, :, :].rearrange("p h n -> p (h n)"), o_ps[t][:, :],
                                        o_hi[:, t, :, :].rearrange("p h n -> p (h n)").bitcast(f32),
                                        ALU.subtract).then_inc(olo_done, 1)

            def x2_low(j):
                dve.wait_ge(x2hi_done, j + 1)
                nc.vector.tensor_tensor(x2_view(x2_lo, j), xt2_src(), x2_view(x2_hi, j).bitcast(f32),
                                        ALU.subtract).then_inc(x2lo_done, 1)

            def log_sigmoid(j):
                dve.wait_ge(ln_done, j + 1)
                need(dve, cum_done, j)
                nc.vector.scalar_tensor_tensor(gk[:, :, :].rearrange("p a b -> p (a b)"), z_ps[:, :], 0.0,
                                               lsig[:, :], ALU.min, ALU.subtract).then_inc(gk_done, 1)

            def second_residual(j):
                dve.wait_ge(wo_done, j + 1)
                rows = Hres[:, bass.ds(2 * j, 2), :]
                nc.vector.tensor_tensor(rows, rows, wo_ps[:, :].rearrange("p (t d) -> p t d", t=2), ALU.add).then_inc(h2_done, 1)

            def second_norm(j):
                need(dve, mv2_done, j)
                wait_apart(dve, h2_done, j + 1, dve_passed)
                norm(Hres, j, stats2, mv2, bn2_done, mv2_done, rstd2_done, xn2_done)

            def gated_qk(j):
                dve.wait_ge(epos_done, j + 1)
                dve.wait_ge(q_done, j + 1)
                need(dve, a_done, j)
                nc.vector.tensor_tensor(qg[:, :, :].rearrange("p k n -> p (k n)"), q_ps[:, :],
                                        e_pos[:, :, :].rearrange("p k n -> p (k n)"), ALU.mult).then_inc(qg_done, 1)
                dve.wait_ge(eneg_done, j + 1)
                dve.wait_ge(k_done, j + 1)
                nc.vector.tensor_tensor(kg[:, :, :].rearrange("p k n -> p (k n)"), k_ps[:, :],
                                        e_neg[:, :, :].rearrange("p k n -> p (k n)"), ALU.mult).then_inc(kg_done, 1)

            def open_lr_low(t):
                cols = slice(t * S, (t + 1) * S)
                dve.wait_ge(of(t, opening["lrx_hi"], lrx_hi_done), 1)
                nc.vector.tensor_tensor(lr_x[BLK:BLK + RANK, 0, cols], lr_in_bank(open_lr[t])[:, 0, cols],
                                        lr_x[0:RANK, 0, cols].bitcast(f32), ALU.subtract).then_inc(
                    of(t, opening["lrx_lo"], lrx_lo_done), 1)

            def open_h(t):
                dve.wait_ge(of(t, opening["lora"], lora_done), 1)
                dve.wait_ge(open_gathered[t], 16)
                nc.vector.tensor_tensor(Hres[:, t, :], open_G[:, t, 0:D], open_lora[t][:, t * D:(t + 1) * D],
                                        ALU.add).then_inc(of(t, opening["h"], h_done), 1)

            def one_bn(stats, t, row, ready, count, done):
                wait_apart(dve, ready, count, dve_passed)
                nc.vector.bn_stats(stats[:, t, :], Hres[:, row, :]).then_inc(done, 1)

            def one_aggr(mv, stats, t, ready, count, done):
                wait_apart(dve, ready, count, dve_passed)
                nc.vector.bn_aggr(mv[:, t, :], stats[:, t, :]).then_inc(done, 1)

            def one_normed(dst, t, row, mv, rstd, ready, count, done):
                dve.wait_ge(ready, count)
                nc.vector.tensor_scalar(dst[:, t, :], Hres[:, row, :], mv[:, t, 0:1], rstd[:, t:t + 1],
                                        ALU.subtract, ALU.mult).then_inc(done, 1)

            open_lr_low(0)
            open_h(0)
            open_lr_low(1)
            for t in range(2):
                one_bn(stats, t, t, of(t, opening["h"], h_done), 1, of(t, opening["bn"], bn_done))
                if t == 0:
                    open_h(1)
                one_aggr(mv, stats, t, of(t, opening["bn"], bn_done), 1, of(t, opening["mv"], mv_done))
            for t in range(2):
                one_normed(xn, t, t, mv, rstd, of(t, opening["rstd"], rstd_done), 1, of(t, opening["xn"], xn_done))
            for t in range(2):
                cols = slice(t * S, (t + 1) * S)
                dve.wait_ge(of(t, opening["xhi"], xhi_done), 1)
                last = nc.vector.tensor_tensor(x_lo[:, :, cols], seqs_of(open_xt[t], t), x_hi[:, :, cols].bitcast(f32),
                                               ALU.subtract)
            last.then_inc(xlo_done, 1)

            def step(i):
                en, fw, bk, cc = i + 1, i, i - 1, i - 2
                if on(fw) and not opened(fw):
                    dve.wait_ge(xhi_done, fw + 1)
                    nc.vector.tensor_tensor(x_lo[:, :, :].rearrange("p k n -> p (k n)"), xt_ps[:, :],
                                            x_hi[:, :, :].rearrange("p k n -> p (k n)").bitcast(f32),
                                            ALU.subtract).then_inc(xlo_done, 1)
                if isinstance(i, int) and i == 0:
                    wa_low(2, slice(WQK, WCOLS))
                if on(bk):
                    mask_scores(bk)
                if on(cc):
                    second_residual(cc)
                    second_norm(cc)
                parts = rank_parts(i)
                if parts:
                    dve.wait_ge(lrx_hi_done, i + 2)
                    nc.vector.tensor_tensor(lr_x[BLK:BLK + RANK, parts, :], lr_ps[:, parts, :],
                                            lr_x[0:RANK, parts, :].bitcast(f32), ALU.subtract).then_inc(lrx_lo_done, 1)
                if on(cc):
                    second_normed(cc)
                if on(en):
                    j = en
                    dve.wait_ge(lora_done, j + 1)
                    for t in range(2):
                        dve.wait_ge(gathered[t], 16 * j)
                    nc.vector.tensor_tensor(Hres[:, bass.ds(2 * j, 2), :], G[:, :, 0:D],
                                            lora_ps[:, :].rearrange("p (t d) -> p t d", t=2), ALU.add).then_inc(h_done, 1)
                    need(dve, mv_done, j)
                    wait_apart(dve, h_done, j + 1, dve_passed)
                    norm(Hres, j, stats, mv, bn_done, mv_done, rstd_done, xn_done)

                if late(fw):
                    log_sigmoid(fw)
                if on(bk):
                    sums(bk, 0)
                if on(cc):
                    x2_low(cc)
                if late(fw):
                    sums(bk, 1)
                    gated(bk, 0)
                    gated_qk(fw)
                    gated(bk, 1)
                    o_low(bk, 0)
                else:
                    log_sigmoid(fw)
                    if on(bk):
                        gated(bk, 0)
                        sums(bk, 1)
                    j = en
                    dve.wait_ge(rstd_done, j + 1)
                    need(dve, xt_done, j)
                    normed(xn, Hres, j, mv, rstd, xn_done)
                    if on(bk):
                        o_low(bk, 0)
                        gated(bk, 1)
                    gated_qk(fw)
                    if on(bk):
                        o_low(bk, 1)
                if first_chunk(i):
                    c = i - 2
                    rows = slice(0, rows2(c) if isinstance(c, int) else P)
                    cols = first2(c)
                    dve.wait_ge(w2_hi_done, c + 1)
                    nc.vector.tensor_tensor(e_lo[rows, cols], raw[0][rows, cols], e_hi[rows, cols].bitcast(f32),
                                            ALU.subtract).then_inc(w2_lo_done, 1)
                if isinstance(i, int) and i == 0:
                    dve.wait_ge(wo_in, 16)
                    dve.wait_ge(gn_in, 16)
                    nc.vector.tensor_scalar(wo_raw, wo_raw, gn_sb[:, 0:1], None, ALU.mult).then_inc(wo_scaled, 1)
                    dve.wait_ge(wo_scaled, 1)
                    nc.vector.tensor_copy(wo_hi2, wo_raw).then_inc(wo_hi_done, 1)
                    dve.wait_ge(wo_hi_done, 1)
                    nc.vector.tensor_tensor(wo_lo2, wo_raw, wo_hi2.bitcast(f32), ALU.subtract).then_inc(wa_lo_done, 1)

            steps(dve, step)

            L, M = NP - 1, NP - 2
            mask_scores(L)
            o_low(M, 1)
            sums(L, 0)
            sums(L, 1)
            gated(L, 0)
            gated(L, 1)
            second_residual(M)
            o_low(L, 0)
            o_low(L, 1)
            second_norm(M)

            def close_h2(t):
                dve.wait_ge(closing["wo"], t + 1)
                nc.vector.tensor_tensor(Hres[:, 2 * L + t, :], Hres[:, 2 * L + t, :], close_wo[t][:, t * D:(t + 1) * D],
                                        ALU.add).then_inc(of(t, closing["h2"], h2_done), 1)

            close_h2(0)
            one_bn(stats, 0, 2 * L, closing["h2"], 1, closing["bn"])
            close_h2(1)
            one_aggr(mv, stats, 0, closing["bn"], 1, closing["mv"])
            one_bn(stats, 1, 2 * L + 1, h2_done, NP, closing["bn"])
            second_normed(M)
            one_aggr(mv, stats, 1, closing["bn"], 2, closing["mv"])
            for t in range(2):
                one_normed(xn, t, 2 * L + t, mv, rstd, closing["rstd"], t + 1, closing["xn"])
            x2_low(M)
            for t in range(2):
                dve.wait_ge(closing["x2hi"], t + 1)
                last = nc.vector.tensor_tensor(x2_view(x2_lo, L)[:, t::2], xt2_src(close_xt2[t])[:, t::2],
                                               x2_view(x2_hi, L)[:, t::2].bitcast(f32), ALU.subtract)
            last.then_inc(x2lo_done, 1)

            def w2_low(e, s, c):
                a, n = chunk2(c)
                r = rows2(c)
                dve.wait_ge(w2_hi_done, (e + 1) * FC + c + 1)
                nc.vector.tensor_tensor(e_lo[0:r, a:a + n], raw[1 - s][0:r, a:a + n],
                                        e_hi[0:r, a:a + n].bitcast(f32), ALU.subtract).then_inc(w2_lo_done, 1)

            def result(e, s):
                dve.wait_ge(down_done, (e + 1) * FC)
                dve.wait_ge(res_in[s], slot_count(e, s))
                dve.wait_ge(stored[s], slot_count(e, s))
                for t in range(2):
                    last = nc.vector.tensor_tensor(y_out[:, s, t * D:(t + 1) * D], y_ps[t][:, 0:D],
                                                   h_res[:, s, t * D:(t + 1) * D], ALU.add)
                last.then_inc(y_done, 1)

            def expert(e, s, before=True, after=True):
                for c in range(FC):
                    n = e * FC + c
                    r = rows2(c)
                    w = c % 3 * ET
                    if c == 1 and before:
                        result(e - 1, 1 - s)
                    dve.wait_ge(act_done, n + 1)
                    need(dve, hlo_done, n - 2)
                    up = gu_ps[c % 3][:, ET:2 * ET] if r == P else gu_ps[c % 3][FT:2 * FT, 0:ET]
                    nc.vector.tensor_tensor(h32[0:r, w:w + ET], s_act[0:r, w:w + ET], up, ALU.mult).then_inc(mul_done, 1)
                    dve.wait_ge(mul_done, n + 1)
                    need(dve, down_done, n - 2)
                    nc.vector.tensor_copy(h_hi[0:r, w:w + ET], h32[0:r, w:w + ET]).then_inc(hhi_done, 1)
                    dve.wait_ge(hhi_done, n + 1)
                    low = h_lo[:, w:w + ET] if r == P else h_hi[FT:2 * FT, w:w + ET]
                    nc.vector.tensor_tensor(low, h32[0:r, w:w + ET],
                                            h_hi[0:r, w:w + ET].bitcast(f32), ALU.subtract).then_inc(hlo_done, 1)
                    if c >= 2 and after:
                        w2_low(e, s, c - 2)
                    if c < 2 and before:
                        w2_low(e - 1, 1 - s, FC - 2 + c)

            expert(0, 0, before=False)
            expert(1, 1)
            with dve.Fori(1, E // 2 - 1) as pair:
                for s in range(2):
                    expert(pair * 2 + s, s)
            expert(E - 2, 0)
            expert(E - 1, 1, after=False)
            result(E - 1, 1)

        @block.tensor
        def _(pe):
            mm = nc.tensor.matmul

            def split_mm(out, w_pairs, x_pairs):
                n = len(w_pairs)
                for k, ((wh, wl), (xh, xl)) in enumerate(zip(w_pairs, x_pairs)):
                    mm(out, wh, xh, start=k == 0, stop=False)
                    mm(out, wh, xl, start=False, stop=False)
                    last = mm(out, wl, xh, start=False, stop=k == n - 1)
                return last

            COL_Q, COL_K, COL_G, COL_V = RANK, RANK + D, RANK + 2 * D, RANK + 2 * D + NV

            def weights(c0, n):
                return [(wa_hi[:, k, c0:c0 + n], wa_lo[:, k, c0:c0 + n]) for k in range(KT)]

            def tokens(c0, n):
                return [(x_hi[:, k, c0:c0 + n], x_lo[:, k, c0:c0 + n]) for k in range(KT)]

            pe.wait_ge(consts, 9)

            def output_projection(j, t, wo_ps=wo_ps):
                if isinstance(j, int) and j == 0:
                    pe.wait_ge(wa_lo_done, 3)
                if late(j):
                    pe.wait_ge(silu_done, 2 * NP)
                else:
                    pe.wait_ge(silu_done, least(2 * j + 3, 2 * NP - 2))
                pe.wait_ge(olo_done, 2 * j + t + 1)
                return split_mm(wo_ps[:, t * D:(t + 1) * D],
                                [(o_hi[:, t, h, :], o_lo[:, t, h, :]) for h in range(H)],
                                [(wo_hi[:, h, :], wo_lo[:, h, :]) for h in range(H)])

            def xt2(j):
                pe.wait_ge(xn2_done, j + 1)
                pe.wait_ge(lrx_lo_done, least(j + 4, NP + 1))
                need(pe, x2lo_done, j)
                for t in range(2):
                    for k in range(KT):
                        last = nc.tensor.transpose(xt2_ps[:, k * PT + t * S:k * PT + (t + 1) * S],
                                                   xn2[:, t, k * P:(k + 1) * P], ident[:, :])
                last.then_inc(xt2_done, 1)

            def values(j, t):
                pe.wait_ge(am_done, 2 * j + 2)
                if t == 0:
                    need(pe, xlo_done, least(j + 2, NP))
                    need(pe, olo_done, 2 * j - 1)
                else:
                    need(pe, olo_done, 2 * j)
                for h in range(H):
                    last = mm(o_ps[t][:, h * DV:(h + 1) * DV], am[:, h % 2, t, h // 2, :],
                              v_sb[:, t, h * DV:(h + 1) * DV], start=True, stop=True)
                last.then_inc(pv_done, 1)

            def output_gate(j, t):
                if isinstance(j, int) and j == 0:
                    pe.wait_ge(wa_lo_done, 2)
                if late(j):
                    pe.wait_ge(kg_done, NP)
                elif t == 0:
                    need(pe, h_done, least(j + 2, NP))
                    need(pe, h2_done, j - 1)
                else:
                    pe.wait_ge(lrx_lo_done, j + 2)
                    need(pe, x2lo_done, j - 1)
                split_mm(gate_bank(j, t)[:, :], tokens(t * S, S), weights(COL_G, NV)).then_inc(g_done, 1)

            def v_proj(j, t):
                if t == 0:
                    need(pe, am_done, 2 * j)
                else:
                    pe.wait_ge(v_copied, 2 * j + 1)
                split_mm(v_ps[:, :], tokens(t * S, S), weights(COL_V, NV)).then_inc(v_done, 1)

            def o_transpose(j, t):
                pe.wait_ge(og_done, 2 * j + t + 1)
                for h in range(H):
                    last = nc.tensor.transpose(o_ps[t][:, h * P:(h + 1) * P], og[:, t, h * DV:(h + 1) * DV], ident[:, :])
                last.then_inc(ot_done, 1)

            def gates(j):
                pe.wait_ge(lrx_dup_done, j + 2)
                pe.wait_ge(lrx_lo_done, j + 2)
                need(pe, am_done, 2 * j - 1)
                for t in range(2):
                    last = mm(z_ps[:, t * D:(t + 1) * D], lr_x[0:LK, 1, t * S:(t + 1) * S], lr_w[0:LK, 1, :],
                              start=True, stop=True)
                last.then_inc(z_done, 1)

            def scores(j):
                pe.wait_ge(kg_done, j + 1)
                pe.wait_ge(v_copied, 2 * j + 2)
                for t in range(2):
                    for m in range(2):
                        for r in range(2):
                            rows = slice(r * DK, (r + 1) * DK)
                            cols = slice((t * 2 + m) * P, (t * 2 + m + 1) * P)
                            last = mm(a_ps[r][:, cols], kg[rows, m, t * S:(t + 1) * S],
                                      qg[rows, m, t * S:(t + 1) * S], start=True, stop=True)
                last.then_inc(a_done, 1)

            for t in range(2):
                cols = slice(t * S, (t + 1) * S)
                pe.wait_ge(open_gathered[t], 16)
                nc.tensor.transpose(lr_in_bank(open_lr[t])[:, 0, cols], open_G[:, t, D:TW], ident[:, :]).then_inc(
                    of(t, opening["lrx"], lrx_done), 1)
                if t == 0:
                    pe.wait_ge(lr_lo_done, 1)
                pe.wait_ge(of(t, opening["lrx_dup"], lrx_dup_done), 1)
                pe.wait_ge(of(t, opening["lrx_lo"], lrx_lo_done), 1)
                mm(open_lora[t][:, t * D:(t + 1) * D], lr_x[0:LK, 0, cols], lr_w[0:LK, 0, :],
                   start=True, stop=True).then_inc(of(t, opening["lora"], lora_done), 1)
            for t in range(2):
                pe.wait_ge(of(t, opening["xn"], xn_done), 1)
                for k in range(KT):
                    last = nc.tensor.transpose(open_xt[t][:, k * PT + t * S:k * PT + (t + 1) * S],
                                               xn[:, t, k * P:(k + 1) * P], ident[:, :])
                last.then_inc(of(t, opening["xt"], xt_done), 1)

            def step(i):
                en, fw, bk, cc = i + 1, i, i - 1, i - 2
                if on(fw) and not opened(fw):
                    j = fw
                    pe.wait_ge(xn_done, j + 1)
                    need(pe, olo_done, 2 * j - 3)
                    for t in range(2):
                        for k in range(KT):
                            last = nc.tensor.transpose(xt_ps[:, k * PT + t * S:k * PT + (t + 1) * S],
                                                       xn[:, t, k * P:(k + 1) * P], ident[:, :])
                    last.then_inc(xt_done, 1)

                def lora():
                    j = en
                    pe.wait_ge(lrx_dup_done, i + 2)
                    pe.wait_ge(lrx_lo_done, i + 2)
                    need(pe, h2_done, j - 2)
                    for t in range(2):
                        last = mm(lora_ps[:, t * D:(t + 1) * D], lr_x[0:LK, 0, t * S:(t + 1) * S], lr_w[0:LK, 0, :],
                                  start=True, stop=True)
                    last.then_inc(lora_done, 1)

                if on(cc):
                    output_projection(cc, 0)
                if on(bk):
                    scores(bk)
                if on(cc):
                    output_projection(cc, 1).then_inc(wo_done, 1)
                if on(en):
                    j = en
                    for t in range(2):
                        pe.wait_ge(gathered[t], 16 * j)
                    need(pe, silu_done, 2 * i)
                    need(pe, lrx_lo_done, i + 1)
                    for t in range(2):
                        nc.tensor.transpose(lr_ps[:, 0, t * S:(t + 1) * S], G[:, t, D:TW], ident[:, :])
                if on(fw):
                    j = fw
                    pe.wait_ge(xlo_done, j + 1)
                    if isinstance(j, int) and j == 0:
                        pe.wait_ge(wa_lo_done, 1)
                    need(pe, silu_done, 2 * j)
                    split_mm(lr_ps[:, 1, :], weights(0, RANK), tokens(0, PT)).then_inc(lrx_done, 1)
                    need(pe, qg_done, j)
                    for m in range(KT):
                        last = split_mm(q_ps[:, m * PT:(m + 1) * PT], weights(COL_Q + m * P, P), tokens(0, PT))
                    last.then_inc(q_done, 1)
                    need(pe, kg_done, j)
                    for m in range(KT):
                        last = split_mm(k_ps[:, m * PT:(m + 1) * PT], weights(COL_K + m * P, P), tokens(0, PT))
                    last.then_inc(k_done, 1)
                if on(en):
                    lora()
                if late(fw):
                    gates(fw)
                if on(bk):
                    values(bk, 0)
                if on(cc):
                    xt2(cc)
                if on(fw) and not late(fw):
                    gates(fw)
                if on(fw):
                    j = fw
                    if not on(bk):
                        v_proj(fw, 0)
                    if not late(fw):
                        output_gate(j, 0)
                if on(bk):
                    values(bk, 1)
                if on(fw) and on(bk):
                    v_proj(fw, 0)
                if on(fw):
                    j = fw
                    pe.wait_ge(gk_done, j + 1)
                    for t in range(2):
                        for m in range(KT):
                            last = mm(cum_ps[:, m * PT + t * S:m * PT + (t + 1) * S], gk[:, t, m * P:(m + 1) * P],
                                      cum_w[:, :], start=True, stop=True)
                    last.then_inc(cum_done, 1)
                if late(fw):
                    v_proj(fw, 1)
                    o_transpose(bk, 0)
                else:
                    if on(bk):
                        o_transpose(bk, 0)
                    v_proj(fw, 1)
                    output_gate(fw, 1)
                    if on(bk):
                        o_transpose(bk, 1)

            steps(pe, step)

            L, M = NP - 1, NP - 2
            scores(L)
            o_transpose(M, 1)
            output_projection(M, 0)
            values(L, 0)
            values(L, 1)
            output_gate(L, 0)
            output_gate(L, 1)
            output_projection(M, 1).then_inc(wo_done, 1)
            o_transpose(L, 0)
            o_transpose(L, 1)
            for t in range(2):
                output_projection(L, t, close_wo[t]).then_inc(closing["wo"], 1)
            xt2(M)
            for t in range(2):
                pe.wait_ge(closing["xn"], t + 1)
                for k in range(KT):
                    last = nc.tensor.transpose(close_xt2[t][:, k * PT + t * S:k * PT + (t + 1) * S],
                                               xn[:, t, k * P:(k + 1) * P], ident[:, :])
                last.then_inc(closing["xt2"], 1)

            pe.wait_ge(x2lo_done, NP)

            def up(e, c):
                n = e * FC + c
                pe.wait_ge(w13_lo_done, n + 1)
                need(pe, mul_done, n - 2)
                a, _ = chunk13(c)
                xs = [(x2_hi[:, bass.ds(e * KT * ET + k * ET, ET)], x2_lo[:, bass.ds(e * KT * ET + k * ET, ET)])
                      for k in range(KT)]
                parts = 2 if c < FC - 1 else 1
                for g in range(parts):
                    at = [a + k * parts * P + g * P for k in range(KT)]
                    last = split_mm(gu_ps[c % 3][:, g * ET:(g + 1) * ET],
                                    [(e_hi[:, o:o + P], e_lo[:, o:o + P]) for o in at], xs)
                last.then_inc(up_done, 1)

            def down(e, c):
                n = e * FC + c
                r = rows2(c)
                a, _ = chunk2(c)
                pe.wait_ge(hlo_done, n + 1)
                pe.wait_ge(w2_lo_done, n + 1)
                if c == 0:
                    need(pe, y_done, e)
                for t in range(2):
                    w = c % 3 * ET + t * P
                    h, y = slice(w, w + P), y_ps[t][:, 0:D]
                    mm(y, h_hi[:, h], e_hi[:, a:a + D], start=c == 0, stop=False)
                    last = mm(y, h_hi[0:r, h], e_lo[0:r, a:a + D], start=False, stop=c == FC - 1)
                    if c < FC - 1:
                        last = mm(y, h_lo[:, h], e_hi[:, a:a + D], start=False, stop=False)
                last.then_inc(down_done, 1)

            def expert(e, s, before=True):
                for c in range(FC):
                    up(e, c)
                    if c >= 2:
                        down(e, c - 2)
                    elif before:
                        down(e - 1, FC - 2 + c)

            expert(0, 0, before=False)
            expert(1, 1)
            with pe.Fori(1, E // 2) as pair:
                for s in range(2):
                    expert(pair * 2 + s, s)
            down(E - 1, FC - 2)
            down(E - 1, FC - 1)


def kernel(x, L0_tok_base_weight, L0_tok_lora_A, L0_tok_lora_B, L0_attn_Wq, L0_attn_Wk, L0_attn_Wv,
           L0_attn_Wg, L0_attn_gk_w1, L0_attn_gk_w2, L0_attn_gk_b2, L0_attn_g_norm_w, L0_attn_Wo,
           L0_ffn_w1, L0_ffn_w3, L0_ffn_w2):
    import numpy as np
    import concourse.bacc as bacc
    from concourse.bass_utils import run_bass_kernel_spmd

    def a(v):
        return np.asarray(v)

    def chunks(w):
        w = a(w).reshape(E, KT, P, F)
        full = w[:, :, :, :(FC - 1) * P].reshape(E, KT, P, FC - 1, P).transpose(0, 2, 3, 1, 4)
        return full, w[:, :, :, (FC - 1) * P:].transpose(0, 2, 1, 3)

    (f1, t1), (f3, t3) = chunks(L0_ffn_w1), chunks(L0_ffn_w3)
    w13 = np.concatenate([np.stack([f1, f3], 4).reshape(E, P, -1), np.stack([t1, t3], 3).reshape(E, P, -1)], 2)
    w2 = a(L0_ffn_w2)
    w2 = np.concatenate([w2] + [w2[:, (FC - 1) * P:]] * (P // FT - 1), 1).reshape(E, FC, P, D).transpose(0, 2, 1, 3).reshape(E, P, -1)
    low_rank = np.zeros((3, BLK, 2, D), a(L0_tok_lora_B).dtype)
    low_rank[:, :RANK, 0] = a(L0_tok_lora_B)
    low_rank[:, :RANK, 1] = a(L0_attn_gk_w2)
    low_rank[0::2, RANK, 1] = a(L0_attn_gk_b2)
    low_rank = low_rank.reshape(3 * BLK, 2 * D)
    arrays = {
        "ids": a(x).T,
        "table": np.concatenate([a(L0_tok_base_weight).T, a(L0_tok_lora_A)], 1),
        "w_attn": np.concatenate([a(L0_attn_gk_w1), a(L0_attn_Wq), a(L0_attn_Wk), a(L0_attn_Wg), a(L0_attn_Wv)], 1),
        "w_o": a(L0_attn_Wo),
        "low_rank": low_rank,
        "g_norm": a(L0_attn_g_norm_w)[:, None],
        "w13": w13,
        "w2": w2,
    }
    arrays = {k: np.ascontiguousarray(v) for k, v in arrays.items()}
    nc = bacc.Bacc("TRN2", target_bir_lowering=False, num_devices=1)
    args = [nc.dram_tensor(k, v.shape, mybir.dt.from_np(v.dtype), kind="ExternalInput").ap() for k, v in arrays.items()]
    scratch = nc.dram_tensor("scratch", [2, S, B // 2, D], mybir.dt.float32, kind="Internal").ap()
    out = nc.dram_tensor("out", [E, P, 2 * D], mybir.dt.float32, kind="ExternalOutput").ap()
    layer_kernel(nc, *args, scratch, out)
    r = run_bass_kernel_spmd(nc, [arrays], core_ids=[0])
    y = r.results[0]["out"].reshape(E, POS, B // 2, 2, D)
    return np.ascontiguousarray(y.transpose(2, 3, 0, 1, 4)).reshape(B, S, D)
```
